# Optimizing a Trainium2 kernel written in Bass

```python
import numpy as np
import jax
import jax.numpy as jnp

def _softmax(x, axis=-1):
    return jax.nn.softmax(x, axis=axis)

def _gelu(x):
    return jax.nn.gelu(x, approximate=True)

def _silu(x):
    return jax.nn.silu(x)

def _sigmoid(x):
    return jax.nn.sigmoid(x)

def _layernorm(x, axis=-1, eps=1e-05):
    m = jnp.mean(x, axis=axis, keepdims=True)
    v = jnp.var(x, axis=axis, keepdims=True)
    return (x - m) / jnp.sqrt(v + eps)

def _scatter_add(tgt, idx, src, axis=0):
    return tgt.at[idx].add(src)

def _segment_sum(src, seg, n):
    return jax.ops.segment_sum(src, seg, n)
kernel_name = 'mk_cond_resid_d2_seqx_r2_c85c95'

def setup_inputs(seed: int=0):
    np.random.seed(seed)
    _w = jnp.asarray

    def _rec_inputs():
        import jax
        import jax.numpy as jnp
        _rk = jax.random.key(seed)
        x = -0.0002928 + 1 * jax.random.normal(jax.random.fold_in(_rk, 1), (8, 512, 512), jnp.float32)
        _lenS = 512 - jax.random.randint(jax.random.fold_in(_rk, 7), (8,), 0, max(1, 512 // 4) + 1, jnp.int32)
        _lenS2 = 512 - jax.random.randint(jax.random.fold_in(_rk, 8), (8,), 0, max(1, 512 // 4) + 1, jnp.int32)
        cond_1024 = -0.00356592 + 0.997978 * jax.random.normal(jax.random.fold_in(_rk, 11), (8, 512), jnp.float32)
        return (x, cond_1024)
    x, cond_1024 = _rec_inputs()

    def _L0_cond_setup():
        import jax, jax.numpy as jnp
        import numpy as np
        B, T, D = (128, 32, 512)
        ADA, INTER, RANK = (512, 512, 8)
        LN_EPS = 1e-05

        def _layernorm(x, g, b):
            mu = jnp.mean(x, axis=-1, keepdims=True)
            var = jnp.var(x, axis=-1, keepdims=True)
            return (x - mu) * jax.lax.rsqrt(var + LN_EPS) * g + b
        key = jax.random.key(seed)
        ks = jax.random.split(key, 9)
        return {'x': jax.random.normal(ks[0], (B, T, D), dtype=jnp.float32), 'ada_emb': jax.random.normal(ks[1], (B, ADA), dtype=jnp.float32), 'base_layer': jax.random.normal(ks[2], (D, D), dtype=jnp.float32), 'w1': jax.random.normal(ks[3], (ADA, INTER), dtype=jnp.float32) * 0.02, 'b1': jnp.zeros((INTER,), dtype=jnp.float32), 'w2': jax.random.normal(ks[4], (INTER, 2 * D * RANK), dtype=jnp.float32) * 0.02, 'b2': jnp.zeros((2 * D * RANK,), dtype=jnp.float32), 'ln_g': jnp.ones((ADA,), dtype=jnp.float32), 'ln_b': jnp.zeros((ADA,), dtype=jnp.float32)}
    _L0_cond_all = _L0_cond_setup()
    _L0_cond_in = {k: v for k, v in _L0_cond_all.items() if k in ('base_layer', 'w1', 'b1', 'w2', 'b2', 'ln_g', 'ln_b')}
    del _L0_cond_all

    def _L1_cond_setup():
        import jax, jax.numpy as jnp
        import numpy as np
        D, HS, HE, E, K = (512, 1024, 512, 8, 2)
        B, T = (4, 512)
        N_SHARED = 1
        key = jax.random.key(seed)
        ks = jax.random.split(key, 9)
        g = lambda k, shape, s: jax.random.normal(k, shape, jnp.float32) * s
        return {'x': g(ks[0], (B, T, D), 1.0), 't_emb': g(ks[1], (B, D), 1.0), 'router_W': g(ks[2], (2 * D, E), 0.01), 'router_bias': jnp.zeros((E,), jnp.float32), 'w1': g(ks[3], (D, HS), 0.02), 'w3': g(ks[4], (D, HS), 0.02), 'w2': g(ks[5], (HS, D), 0.02), 'W1e': g(ks[6], (E, D, HE), 0.02), 'W2e': g(ks[7], (E, HE, D), 0.02)}
    _L1_cond_all = _L1_cond_setup()
    _L1_cond_in = {k: v for k, v in _L1_cond_all.items() if k in ('router_W', 'router_bias', 'w1', 'w3', 'w2', 'W1e', 'W2e')}
    del _L1_cond_all
    return {'x': x, 'cond_1024': cond_1024, 'L0_cond_base_layer': _L0_cond_in['base_layer'], 'L0_cond_w1': _L0_cond_in['w1'], 'L0_cond_b1': _L0_cond_in['b1'], 'L0_cond_w2': _L0_cond_in['w2'], 'L0_cond_b2': _L0_cond_in['b2'], 'L0_cond_ln_g': _L0_cond_in['ln_g'], 'L0_cond_ln_b': _L0_cond_in['ln_b'], 'L1_cond_router_W': _L1_cond_in['router_W'], 'L1_cond_router_bias': _L1_cond_in['router_bias'], 'L1_cond_w1': _L1_cond_in['w1'], 'L1_cond_w3': _L1_cond_in['w3'], 'L1_cond_w2': _L1_cond_in['w2'], 'L1_cond_W1e': _L1_cond_in['W1e'], 'L1_cond_W2e': _L1_cond_in['W2e']}

def reference(x, cond_1024, L0_cond_base_layer, L0_cond_w1, L0_cond_b1, L0_cond_w2, L0_cond_b2, L0_cond_ln_g, L0_cond_ln_b, L1_cond_router_W, L1_cond_router_bias, L1_cond_w1, L1_cond_w3, L1_cond_w2, L1_cond_W1e, L1_cond_W2e):
    import jax
    import jax.numpy as jnp

    def _L0_cond_ref(x, ada_emb, base_layer, w1, b1, w2, b2, ln_g, ln_b):
        import jax, jax.numpy as jnp
        import numpy as np
        B, T, D = (128, 32, 512)
        ADA, INTER, RANK = (512, 512, 8)
        LN_EPS = 1e-05

        def _layernorm(x, g, b):
            mu = jnp.mean(x, axis=-1, keepdims=True)
            var = jnp.var(x, axis=-1, keepdims=True)
            return (x - mu) * jax.lax.rsqrt(var + LN_EPS) * g + b
        b, t, d = x.shape
        ae = _layernorm(ada_emb, ln_g, ln_b)
        h = jax.nn.gelu(ae @ w1 + b1, approximate=False)
        xw = h @ w2 + b2
        x_a, x_b = jnp.split(xw, 2, axis=-1)
        x_a = x_a.reshape(b, d, RANK)
        x_b = x_b.reshape(b, d, RANK)
        layer = base_layer[None, :, :] + jnp.einsum('bdr,bkr->bdk', x_a, x_b)
        out = jnp.einsum('btc,bco->bto', x, layer)
        return x + out

    def _L1_cond_ref(x, t_emb, router_W, router_bias, w1, w3, w2, W1e, W2e):
        import jax, jax.numpy as jnp
        import numpy as np
        D, HS, HE, E, K = (512, 1024, 512, 8, 2)
        B, T = (4, 512)
        N_SHARED = 1
        Bb, Tt, C = x.shape
        xf = x.reshape(-1, C)
        tf = jnp.broadcast_to(t_emb[:, None, :], (Bb, Tt, C)).reshape(-1, C)
        N = xf.shape[0]
        shared = jax.nn.silu(xf @ w1) * (xf @ w3) @ w2
        s = jax.nn.sigmoid((jnp.concatenate([xf, tf], axis=-1) @ router_W).astype(jnp.float32))
        sel_scores = s + router_bias
        _, topk_idx = jax.lax.top_k(sel_scores, K)
        s_sel = jnp.take_along_axis(s, topk_idx, axis=1)
        denom = s_sel.sum(axis=1, keepdims=True)
        gates = jnp.where(denom > 1e-09, s_sel / (denom + 1e-09), 1.0 / K).astype(x.dtype)
        combine = jnp.zeros((N, E), x.dtype).at[jnp.arange(N)[:, None], topk_idx].add(gates)
        h = jax.nn.gelu(jnp.einsum('nc,ech->enh', xf, W1e), approximate=False)
        y = jnp.einsum('enh,ehc->enc', h, W2e)
        routed = jnp.einsum('ne,enc->nc', combine, y)
        return ((shared + routed) / (N_SHARED + K)).reshape(Bb, Tt, C)
    x = x + _L0_cond_ref(x, cond_1024, L0_cond_base_layer, L0_cond_w1, L0_cond_b1, L0_cond_w2, L0_cond_b2, L0_cond_ln_g, L0_cond_ln_b)
    x = x + _L1_cond_ref(x, cond_1024, L1_cond_router_W, L1_cond_router_bias, L1_cond_w1, L1_cond_w3, L1_cond_w2, L1_cond_W1e, L1_cond_W2e)
    return x

_drawn_inputs = setup_inputs


def setup_inputs(seed=0):
    import zlib

    import numpy as np

    out = dict(_drawn_inputs(seed))
    spreads = {'L0_cond_b1': (0.0, 0.398),
     'L0_cond_b2': (0.0, 0.1),
     'L0_cond_ln_g': (1.0, 0.6),
     'L0_cond_ln_b': (0.0, 0.8),
     'L1_cond_router_bias': (0.0, 1.126)}
    factors = {'L1_cond_router_W': 2.698}
    for name, (base, spread) in spreads.items():
        noise = np.random.default_rng([zlib.crc32(name.encode()), seed]).standard_normal(out[name].shape)
        drawn = base * np.exp(spread * noise) if base else spread * noise
        out[name] = jnp.asarray(drawn.astype(out[name].dtype))
    for name, factor in factors.items():
        out[name] = (out[name] * factor).astype(out[name].dtype)
    return out
```

```python
from contextlib import ExitStack

import concourse.bass as bass
from concourse import mybir

ALU = mybir.AluOpType
ACT = mybir.ActivationFunctionType
F32 = mybir.dt.float32
F32R = mybir.dt.float32r
I32 = mybir.dt.int32
U32 = mybir.dt.uint32
AX = mybir.AxisListType.X
ds = bass.ds

P = 128
TOPK = 2
LN_EPS = 1e-5
GATE_EPS = 1e-9
CH = 512
RING = 3
GROUPS = (0, 32, 64)
ROW, WOFF, WCNT, AROW, FREE, PAD, PAIRS, NACT = range(8)


def build(nc, x, cond, base, cw1, cb1, cw2, cb2, ln_g, ln_b, rw, rb, w1, w3, w2, w1e, w2e, out):
    NB, T, D = x.shape
    KC = D // P
    TT = T // P
    HS = w1.shape[1]
    HC = HS // P
    E, _, HE = w1e.shape
    RK = cw2.shape[1] // (2 * D)
    N = NB * T
    NT = N // P
    REGION = N + P
    ROWS = E * REGION + P
    STACK = GROUPS[-1] + RK
    NCH = cw2.shape[1] // CH
    WPC = CH // RK
    WSL = KC * HE
    HALF = KC // 2
    TILES = (N * TOPK + E * (P - 1)) // P
    PAIRS_MAX = (TILES + 1) // 2
    TAB = -(-(TILES + 5) // 8) * 8
    assert NB == 8 and T == D == HE == CH and TT == KC == 4 and E == 8 and HS == 1024 and RK == 8

    xw_d = nc.dram_tensor("xw_d", (NB, 2, RK, D), F32, kind="Internal").ap()
    x1_d = nc.dram_tensor("x1_d", (N, D), F32, kind="Internal").ap()
    x1T_d = nc.dram_tensor("x1T_d", (P, NB, KC * T), F32, kind="Internal").ap()
    xs_d = nc.dram_tensor("xs_d", (ROWS, D), F32, kind="Internal").ap()
    tab_d = nc.dram_tensor("tab_d", (TAB, 8), I32, kind="Internal").ap()
    ys_d = nc.dram_tensor("ys_d", (PAIRS_MAX * 2 * P, D), F32, kind="Internal").ap()

    x_view = x.rearrange("b (t p) d -> p (b t) d", p=P)
    out_view = out.rearrange("b (t p) d -> p (b t) d", p=P)
    x1_view = x1_d.rearrange("(n p) d -> p n d", p=P)
    w1e_view = w1e.rearrange("e (k p) n -> p (e k) n", p=P)
    w2e_view = w2e.rearrange("e (k p) n -> p (e k) n", p=P)
    cw2_view = cw2.rearrange("(k p) n -> p k n", p=P)

    def row_bc(v, parts):
        return v.rearrange("(a n) -> a n", a=1).broadcast_to([parts, v.shape[0]])

    with ExitStack() as ctx:
        def sb(name, shape, dt=F32, where=ctx):
            return where.enter_context(nc.sbuf_tensor(name, shape, dt))

        def sem(name):
            return ctx.enter_context(nc.semaphore(name))

        M = [ctx.enter_context(nc.psum_tensor(f"M{i}", [P, CH], F32)) for i in range(4)]
        K = [ctx.enter_context(nc.psum_tensor(f"K{i}", [P, CH], F32)) for i in range(2)]
        L = ctx.enter_context(nc.psum_tensor("L", [P, CH], F32))
        Rb = ctx.enter_context(nc.psum_tensor("Rb", [P, CH], F32))
        U = K
        V = [L, Rb]
        TX, TH, HP, YP = K[0], K[1], L, Rb

        w13h = sb("w13h", [P, 2, KC, HS], F32R)
        w13l = sb("w13l", [P, 2, KC, HS], F32R)
        w2h = sb("w2h", [P, HC, D], F32R)
        w2l = sb("w2l", [P, HC, D], F32R)
        ident = sb("ident", [P, P])
        upper = sb("upper", [P, P])
        ones = sb("ones", [P, P])
        zeros = sb("zeros", [P, P])
        iota8 = sb("iota8", [P, E])
        iotap = sb("iotap", [P, 1])
        tb = sb("tb", [P, NB, E])
        rbias = sb("rbias", [P, E])
        rwhl = sb("rwhl", [P, KC, 2 * E], F32R)
        pos_all = sb("pos_all", [P, NT * TOPK])
        ypos = sb("ypos", [P, NT * TOPK], I32)
        gate_all = sb("gate_all", [P, NT * TOPK])
        pos_fix = sb("pos_fix", [P, 2, TT * TOPK], I32)
        gate_fix = sb("gate_fix", [P, TT * TOPK])
        tabi = sb("tabi", [P, 8], I32)
        tab = sb("tab", [P, 8])
        tab_i = sb("tab_i", [1, TAB * 8], I32)
        run = sb("run", [P, TT + 1, E])

        over1 = ExitStack()
        x1h = sb("x1h", [P, KC, T], F32R, over1)
        x1l = sb("x1l", [P, KC, T], F32R, over1)
        over1.close()
        with ExitStack() as over1:
            xgh = sb("xgh", [P, KC, P], F32R, over1)
            xgl = sb("xgl", [P, KC, P], F32R, over1)
            hTh = sb("hTh", [P, KC, P], F32R, over1)
            hTl = sb("hTl", [P, KC, P], F32R, over1)
            hg = sb("hg", [P, HE], F32, over1)
            yo = sb("yo", [P, 2, D], F32, over1)
        over1 = ctx.enter_context(ExitStack())
        sb("over1_hold", [P, 2 * KC * T], F32, over1)

        with ExitStack() as st:
            basep = sb("basep", [P, KC, D], F32, st)
            xtok = sb("xtok", [P, TT, D], F32, st)
            with ExitStack() as z:
                w2c = sb("w2c", [P, RING, KC, CH], F32, z)
                b2c = sb("b2c", [8, RING, CH], F32, z)
                w1c = sb("w1c", [P, KC, D], F32, z)
                wraw = sb("wraw", [P, 2, 2048], F32, z)
                xwc = sb("xwc", [8, 2, RK, WPC], F32, z)
                craw = sb("craw", [8, D], F32, z)
                lng = sb("lng", [8, D], F32, z)
                lnb = sb("lnb", [8, D], F32, z)
                cb1b = sb("cb1b", [8, D], F32, z)
                ae = sb("ae", [8, D], F32, z)
                hc_ = sb("hcond", [8, D], F32, z)
                actT = sb("actT", [P, 3, KC, 8], F32, z)
                stats = sb("stats", [8, 16], F32, z)
                rwr = sb("rwr", [P, 2 * KC, E], F32, z)
                tbs = sb("tbs", [8, NB, E], F32, z)
            xTh = sb("xTh", [P, KC, T], F32R, st)
            xTl = sb("xTl", [P, KC, T], F32R, st)
            layf = sb("layf", [P, 2, D], F32, st)
            layh = sb("layh", [P, KC, D], F32R, st)
            layl = sb("layl", [P, KC, D], F32R, st)
            stkr = sb("stkr", [STACK, 2, D], F32, st)
            stk = sb("stk", [STACK, 2, D], F32R, st)
            x1T = sb("x1T", [P, KC, T], F32, st)
            x1tok = sb("x1tok", [P, 2, TT, D], F32, st)
            rs = [sb(f"rs{i}", [P, TT, TOPK, E], F32, st) for i in range(4)]
            mx = sb("mx", [P, TT, E], F32, st)
            mi = sb("mi", [P, TT, E], U32, st)
            sg = [sb(f"sg{i}", [P, TT * TOPK * 2], F32, st) for i in range(3)]
            msk = sb("msk", [P, TT, TOPK, E], F32, st)
        slf = sb("slf", [P, 2, T])
        gTh = sb("gTh", [P, 2, T], F32R)
        gTl = sb("gTl", [P, 2, T], F32R)
        tw = sb("tw", [P, 12, E])
        twi = sb("twi", [P, 4, E], I32)
        step = sb("step", [P, NT * TOPK])
        slots = sb("slots", [P, NT * TOPK])
        with ExitStack() as st:
            xr = sb("xr", [P, 2, D], F32, st)
            weh = sb("weh", [P, 2, 2 * WSL], F32R, st)
            wel = sb("wel", [P, 2, 2 * WSL], F32R, st)
            weraw = sb("weraw", [P, WSL], F32, st)
        with ExitStack() as st:
            x1raw = sb("x1raw", [P, KC * T], F32, st)
            xres = sb("xres", [P, TT, D], F32, st)
            yb = sb("yb", [P, TT * TOPK, D], F32, st)

        small_in = sem("small_in")
        w2c_in = [sem(f"w2c_in{i}") for i in range(RING)]
        wraw_in = [sem(f"wraw_in{i}") for i in range(2)]
        base_in = sem("base_in")
        consts = sem("consts")
        waited = {e.engine: sem(f"waited_{n}") for n, e in
                  (("sp", nc.sync), ("pool", nc.gpsimd), ("dve", nc.vector), ("act", nc.scalar), ("pe", nc.tensor))}
        d0 = sem("d0")
        p0 = sem("p0")
        a0 = sem("a0")
        xw_ps = sem("xw_ps")
        xw_sb = sem("xw_sb")
        xwc_out = [sem(f"xwc_out{i}") for i in range(2)]
        wsh = sem("wsh")
        wsl = sem("wsl")
        x_in = [sem(f"x_in{c}") for c in range(KC)]
        stk_in = sem("stk_in")
        stk_hi = sem("stk_hi")
        stk_lo = sem("stk_lo")
        xt_ps = sem("xt_ps")
        xt_hi = sem("xt_hi")
        xt_lo = sem("xt_lo")
        lay_ps = sem("lay_ps")
        lay_f = sem("lay_f")
        lay_hi = sem("lay_hi")
        lay_lo = sem("lay_lo")
        main_ps = sem("main_ps")
        x1_f = sem("x1_f")
        x1_hi = sem("x1_hi")
        x1_lo = sem("x1_lo")
        tok_ps = sem("tok_ps")
        tok_sb = sem("tok_sb")
        z_ps = sem("z_ps")
        z_sb = sem("z_sb")
        ez = sem("ez")
        masks = sem("masks")
        rank_ps = sem("rank_ps")
        pos_rdy = sem("pos_rdy")
        dr = sem("dr")
        x1T_out = sem("x1T_out")
        x1_out = [sem(f"x1_out{i}") for i in range(2)]
        scat = [sem(f"scat{i}") for i in range(2)]
        tabs = sem("tabs")
        dt_ = sem("dt")
        pad_out = sem("pad_out")
        class Ffn:
            def __init__(self, tag):
                self.u_ps = sem(f"u_ps_{tag}")
                self.v_ps = sem(f"v_ps_{tag}")
                self.silu = sem(f"silu_{tag}")
                self.g_f = sem(f"g_f_{tag}")
                self.g_hi = sem(f"g_hi_{tag}")
                self.g_lo = sem(f"g_lo_{tag}")
                self.o_ps = sem(f"o_ps_{tag}")
                self.sum_ps = sem(f"sum_ps_{tag}")
        S, F = Ffn("s"), Ffn("f")
        places_all = sem("places_all")
        gates = sem("gates")
        tab_out = sem("tab_out")
        tab_in = sem("tab_in")
        xr_in = [sem(f"xr_in{i}") for i in range(2)]
        xg_ps = sem("xg_ps")
        xg_hi = sem("xg_hi")
        xg_lo = sem("xg_lo")
        h_ps = sem("h_ps")
        h_g = sem("h_g")
        ht_ps = sem("ht_ps")
        ht_hi = sem("ht_hi")
        ht_lo = sem("ht_lo")
        y_ps = sem("y_ps")
        y_sb = sem("y_sb")
        y_out = [sem(f"y_out{i}") for i in range(2)]
        weraw_in = sem("weraw_in")
        we_hi = sem("we_hi")
        we_lo = sem("we_lo")
        x1raw_in = sem("x1raw_in")
        xres_in = sem("xres_in")
        xf_hi = sem("xf_hi")
        xf_lo = sem("xf_lo")
        pos_f = sem("pos_f")
        y_in = sem("y_in")
        gate_f = sem("gate_f")
        acc = sem("acc")
        comb = sem("comb")
        out_st = sem("out_st")

        block = ctx.enter_context(nc.Block())

        N_SMALL = 9
        PIECES = 6
        D_VAR, D_RSTD, D_AE, D_CT, D_AET, D_HPRE, D_HT, D_TBS, D_TB = 3, 4, 7, 8, 9, 10, 11, 14, 15

        def value(eng, col, at, hi, lo=0):
            alone(eng)
            return eng.value_load(tab_i[0:1, ds(at * 8 + col, 1)], min_val=lo, max_val=hi)

        def blocks(eng, body, done):
            for b in range(3):
                body(b, b % 2)
            with eng.Fori(1, (NB - 2) // 2) as i:
                body(i * 2 + 1, 1)
                body(i * 2 + 2, 0)
            body(NB - 1, 1)
            done()

        def tiles(eng, pairs, body):
            body(0)
            with eng.Fori(1, pairs) as j:
                body(j)

        def alone(eng):
            eng.sem_inc(waited[eng.engine], 1)

        def first(b):
            return isinstance(b, int) and b == 0

        def last(b):
            return isinstance(b, int) and b == NB - 1

        def piece_of(w13, w2x, i):
            if i < 4:
                return w13[:, i // 2, (i % 2) * HALF:(i % 2 + 1) * HALF].rearrange("p k n -> p (k n)")
            return w2x[:, (i - 4) * KC:(i - 3) * KC].rearrange("p k n -> p (k n)")

        def flat(a):
            return a.rearrange("p k n -> p (k n)")

        def before(eng, ffn, b, h, none):
            if h >= 2:
                eng.wait_ge(ffn.o_ps, b * (HC - 1) + (h - 1))
            elif not none:
                eng.wait_ge(*((ffn.o_ps, b * (HC - 1)) if h == 0 else (ffn.sum_ps, b * TT)))

        def ffn_act(act, ffn, b, none):
            for h in range(HC):
                n = b * HC + h
                act.wait_ge(ffn.u_ps, n + 1)
                if h >= 2 or not none:
                    act.wait_ge(ffn.g_lo, n - 1)
                nc.scalar.activation(slf[:, h % 2], U[h % 2][:], ACT.Silu).then_inc(ffn.silu, 1)
                act.wait_ge(ffn.g_f, n + 1)
                before(act, ffn, b, h, none)
                nc.scalar.copy(gTh[:, h % 2], slf[:, h % 2]).then_inc(ffn.g_hi, 1)

        def ffn_dve(dve, ffn, b):
            for h in range(HC):
                n = b * HC + h
                dve.wait_ge(ffn.silu, n + 1)
                dve.wait_ge(ffn.v_ps, n + 1)
                nc.vector.tensor_tensor(slf[:, h % 2], V[h % 2][:], slf[:, h % 2], ALU.mult).then_inc(ffn.g_f, 1)
                dve.wait_ge(ffn.g_hi, n + 1)
                nc.vector.tensor_tensor(gTl[:, h % 2], slf[:, h % 2], gTh[:, h % 2].bitcast(F32),
                                        ALU.subtract).then_inc(ffn.g_lo, 1)

        def store_factors(sp, n):
            ab, w0 = n // (NCH // 2), n % (NCH // 2) * WPC
            sp.dma_start(xw_d[:, ab, :, w0:w0 + WPC], xwc[:, n % 2]).then_inc(xwc_out[n % 2], 16)

        def load_piece(sp, shared, i):
            w, half = shared[i]
            if i >= 2:
                sp.wait_ge(wsh, i - 1)
                sp.wait_ge(wsl, i - 1)
            k = w.shape[0] // P // 2
            src = w.rearrange("(k p) n -> p k n", p=P)[:, half * k:(half + 1) * k, :]
            sp.dma_start(wraw[:, i % 2].rearrange("p (k n) -> p k n", k=k), src).then_inc(wraw_in[i % 2], 16)

        def load_stack(sp, b):
            for g in GROUPS:
                sp.dma_start(stkr[g:g + RK], xw_d[ds(b, 1)].rearrange("b a r d -> (b r) a d")
                             ).then_inc(stk_in, 16)

        @block.sync
        def _(sp):
            for dst, src in ((craw[:], cond), (lng[:], row_bc(ln_g, 8)), (lnb[:], row_bc(ln_b, 8)),
                             (w1c[:], cw1.rearrange("(k p) n -> p k n", p=P)),
                             (cb1b[:], row_bc(cb1, 8)),
                             (rwr[:], rw.rearrange("(k p) e -> p k e", p=P)),
                             (rbias[:], row_bc(rb, P))):
                sp.dma_start(dst, src).then_inc(small_in, 16)
            shared = [(w1, 0), (w1, 1), (w3, 0), (w3, 1), (w2, 0), (w2, 1)]
            piece = 0
            for n in range(NCH):
                r = n % RING
                if n >= RING:
                    sp.wait_ge(xw_sb, n - RING + 1)
                sp.dma_start(w2c[:, r], cw2_view[:, :, n * CH:(n + 1) * CH]).then_inc(w2c_in[r], 16)
                sp.dma_start(b2c[:, r], row_bc(cb2[n * CH:(n + 1) * CH], 8)).then_inc(w2c_in[r], 16)
                if n >= 2:
                    sp.wait_ge(xw_sb, n - 1)
                    store_factors(sp, n - 2)
                if n >= 4 and n % 2 == 0 and piece < PIECES:
                    load_piece(sp, shared, piece)
                    piece += 1
            for n in (NCH - 2, NCH - 1):
                sp.wait_ge(xw_sb, n + 1)
                store_factors(sp, n)
            sp.dma_start(basep[:], base.rearrange("(k p) n -> p k n", p=P)).then_inc(base_in, 16)
            for c in range(KC):
                sp.dma_start(xtok[:, :, c * P:(c + 1) * P],
                             x_view[:, 0:TT, c * P:(c + 1) * P]).then_inc(x_in[c], 16)
            while piece < PIECES:
                load_piece(sp, shared, piece)
                piece += 1
            for i in range(2):
                sp.wait_ge(xwc_out[i], 16 * NCH // 2)
            sp.wait_ge(consts, 8)
            load_stack(sp, 0)

            def body(b, slot):
                if not last(b):
                    sp.wait_ge(stk_hi, b + 1)
                    sp.wait_ge(stk_lo, b * 2 + 2)
                    load_stack(sp, b + 1)
                    for c in range(KC):
                        sp.wait_ge(xt_ps, b * KC + c + 1)
                        sp.dma_start(xtok[:, :, c * P:(c + 1) * P],
                                     x_view[:, ds((b + 1) * TT, TT), c * P:(c + 1) * P]).then_inc(x_in[c], 16)
                sp.wait_ge(x1_f, b * KC + KC)
                sp.dma_start(x1T_d[:, ds(b, 1), :].rearrange("p b n -> p (b n)"),
                             x1T[:].rearrange("p k n -> p (k n)")).then_inc(x1T_out, 16)
                sp.wait_ge(tok_sb, b * TT + TT)
                sp.dma_start(x1_view[:, ds(b * TT, TT), :], x1tok[:, slot]).then_inc(x1_out[slot], 16)

            def done():
                zero_src = zeros[:].unsqueeze(1).broadcast_to([P, KC, P])

                def zero_rows(row):
                    return xs_d[ds(row, P), :].rearrange("r (k c) -> r k c", k=KC)
                sp.wait_ge(consts, 8)
                sp.dma_start(zero_rows(E * REGION), zero_src).then_inc(pad_out, 16)
                for t in range(N * TOPK // P, 2 * PAIRS_MAX):
                    sp.dma_start(ys_d[t * P:(t + 1) * P, :].rearrange("r (k c) -> r k c", k=KC), zero_src).then_inc(pad_out, 16)
                sp.wait_ge(tabs, 1)
                sp.dma_start(tab_d, tabi[0:TAB]).then_inc(tab_out, 16)
                sp.wait_ge(tab_out, 16)
                sp.dma_start(tab_i[:], tab_d.rearrange("(a p) c -> a (p c)", a=1)).then_inc(tab_in, 16)
                sp.wait_ge(tab_in, 16)
                with sp.Fori(0, E) as e:
                    row = value(sp, PAD, e, E * REGION - P)
                    sp.dma_start(zero_rows(row), zero_src).then_inc(pad_out, 16)
                sp.wait_ge(pad_out, 16 * (E + 1 + 2 * PAIRS_MAX - N * TOPK // P))
                for s in range(2):
                    sp.wait_ge(scat[s], 16 * TT * TOPK * NB // 2)

            blocks(sp, body, done)
            for s in range(2):
                sp.wait_ge(x1_out[s], 16 * NB // 2)
            sp.wait_ge(x1T_out, 16 * NB)
            def load_rows(t, slot):
                row = value(sp, ROW, t, E * REGION)
                sp.dma_start(xr[:, slot], xs_d[ds(row, P), :]).then_inc(xr_in[slot], 16)
            load_rows(0, 0)
            load_rows(1, 1)
            sp.wait_ge(xg_ps, 1)
            load_rows(2, 0)
            sp.wait_ge(xg_ps, 2)
            load_rows(3, 1)
            pairs = value(sp, PAIRS, 0, PAIRS_MAX, 1)

            def rpair(j):
                for s in range(2):
                    t = j * 2 + s
                    sp.wait_ge(xg_ps, t + 3)
                    load_rows(t + 4, s)
                    sp.wait_ge(y_sb, t + 1)
                    alone(sp)
                    sp.dma_start(ys_d[ds(t * P, P), :], yo[:, s]).then_inc(y_out[s], 16)
            tiles(sp, pairs, rpair)
            for s in range(2):
                sp.wait_ge(xr_in[s], pairs * 16 + 32)
                alone(sp)
            sp.wait_ge(y_ps, pairs * 2 + 1)
            alone(sp)
            sp.dma_start(x1raw[:], x1T_d[:, 0:1, :].rearrange("p b n -> p (b n)")).then_inc(x1raw_in, 16)
            sp.dma_start(xres[:], x1_view[:, (NB - 1) * TT:NB * TT, :]).then_inc(xres_in, 16)
            sp.wait_ge(comb, TT)
            sp.dma_start(out_view[:, (NB - 1) * TT:NB * TT, :], xres[:]).then_inc(out_st, 16)

            def fblock(b, ends):
                sp.wait_ge(out_st, (b + 1) * 16)
                alone(sp)
                sp.dma_start(xres[:], x1_view[:, ds(b * TT, TT), :]).then_inc(xres_in, 16)
                if not ends:
                    sp.wait_ge(xf_hi, b * KC + KC)
                    sp.wait_ge(xf_lo, b * KC + KC)
                    alone(sp)
                    sp.dma_start(x1raw[:], x1T_d[:, ds(b + 1, 1), :].rearrange("p b n -> p (b n)")
                                 ).then_inc(x1raw_in, 16)
                sp.wait_ge(comb, b * TT + 2 * TT)
                alone(sp)
                sp.dma_start(out_view[:, ds(b * TT, TT), :], xres[:]).then_inc(out_st, 16)
            with sp.Fori(0, NB - 2) as b:
                fblock(b, False)
            fblock(NB - 2, True)
            sp.wait_ge(out_st, 16 * NB)

        @block.gpsimd
        def _(pool):
            nc.gpsimd.memset(ident[:], 0.0).then_inc(consts, 1)
            nc.gpsimd.memset(ones[:], 1.0).then_inc(consts, 1)
            pool.wait_ge(consts, 2)
            nc.gpsimd.affine_select(out=ident[:], in_=ident[:], compare_op=ALU.not_equal, fill=1.0, base=0,
                                    pattern=[[-1, P]], channel_multiplier=1).then_inc(consts, 1)
            nc.gpsimd.affine_select(out=upper[:], in_=ones[:], compare_op=ALU.is_gt, fill=0.0, base=0,
                                    pattern=[[1, P]], channel_multiplier=-1).then_inc(consts, 1)
            nc.gpsimd.iota(iota8[:], pattern=[[1, E]], base=0, channel_multiplier=0,
                           allow_small_or_imprecise_dtypes=True).then_inc(consts, 1)
            nc.gpsimd.iota(iotap[:], pattern=[[1, 1]], base=0, channel_multiplier=1,
                           allow_small_or_imprecise_dtypes=True).then_inc(consts, 1)
            nc.gpsimd.memset(zeros[:], 0.0).then_inc(consts, 1)
            pool.wait_ge(xw_ps, NCH)
            pool.wait_ge(xw_sb, NCH)
            pool.wait_ge(p0, 5)
            pool.wait_ge(wsh, PIECES)
            pool.wait_ge(wsl, PIECES)
            nc.gpsimd.memset(stkr[:], 0.0).then_inc(consts, 1)

            def scatter(b, slot):
                pool.wait_ge(pos_rdy, b + 1)
                pool.wait_ge(tok_sb, b * TT + TT)
                alone(pool)
                for t in range(TT):
                    for k in range(TOPK):
                        c = t * TOPK + k
                        pool.indirect_dma_start(
                            out=xs_d, out_offset=bass.IndirectOffsetOnAxis(ap=pos_fix[:, slot, c:c + 1].bitcast(U32), axis=0),
                            in_=x1tok[:, slot, t, :], in_offset=None).then_inc(scat[slot], 16)

            def body(b, slot):
                for c in range(KC):
                    pool.wait_ge(x1_hi, b * KC + c + 1)
                    nc.gpsimd.tensor_tensor(x1l[:, c], x1T[:, c], x1h[:, c].bitcast(F32),
                                            ALU.subtract).then_inc(x1_lo, 1)
                if not first(b):
                    scatter(b - 1, 1 - slot)

            def done():
                scatter(NB - 1, (NB - 1) % 2)

            blocks(pool, body, done)
            pool.wait_ge(tab_in, 16)
            for s in range(2):
                pool.wait_ge(scat[s], 16 * TT * TOPK * NB // 2)
                pool.wait_ge(x1_out[s], 16 * NB // 2)
            pool.wait_ge(x1T_out, 16 * NB)
            nact = value(pool, NACT, 0, E, 2)

            def cut_expert(k):
                arow = value(pool, AROW, k, (E - 1) * KC)
                free = value(pool, FREE, k, P)
                off = (k & 1) * WSL
                pool.wait_ge(y_ps, free + 1)
                for m, view in ((0, w1e_view), (1, w2e_view)):
                    raw = weraw[:].rearrange("p (k n) -> p k n", k=KC)
                    if not (first(k) and m == 0):
                        pool.wait_ge(we_lo, k * 2 + m)
                    alone(pool)
                    pool.dma_start(raw, view[:, ds(arow, KC), :]).then_inc(weraw_in, 16)
                    pool.wait_ge(weraw_in, k * 32 + 16 * m + 16)
                    alone(pool)
                    hi, lo = weh[:, m, ds(off, WSL)], wel[:, m, ds(off, WSL)]
                    nc.gpsimd.tensor_copy(hi, weraw[:]).then_inc(we_hi, 1)
                    pool.wait_ge(we_hi, k * 2 + m + 1)
                    nc.gpsimd.tensor_tensor(lo, weraw[:], hi.bitcast(F32), ALU.subtract).then_inc(we_lo, 1)
            cut_expert(0)
            with pool.Fori(1, nact) as k:
                cut_expert(k)
            pairs = value(pool, PAIRS, 0, PAIRS_MAX, 1)
            pool.wait_ge(tabs, 2)
            for s in range(2):
                pool.wait_ge(y_out[s], pairs * 16)
            pool.wait_ge(y_ps, pairs * 2 + 1)
            alone(pool)

            def gather(b, m):
                nc.gpsimd.tensor_copy(pos_fix[:, 0], ypos[:, ds(b * (TT * TOPK), TT * TOPK)]).then_inc(pos_f, 1)
                pool.wait_ge(pos_f, m + 1)
                if not (isinstance(m, int) and m == 0):
                    pool.wait_ge(comb, m * TT)
                alone(pool)
                for c in range(TT * TOPK):
                    pool.indirect_dma_start(
                        out=yb[:, c, :], out_offset=None, in_=ys_d,
                        in_offset=bass.IndirectOffsetOnAxis(ap=pos_fix[:, 0, c:c + 1].bitcast(U32), axis=0)
                    ).then_inc(y_in, 16)
                pool.wait_ge(y_in, (m + 1) * (16 * TT * TOPK))

            gather(NB - 1, 0)
            with pool.Fori(0, NB - 1) as b:
                gather(b, b + 1)

        @block.scalar
        def _(act):
            act.wait_ge(d0, D_VAR)
            nc.scalar.activation(stats[:, 9:10], stats[:, 8:9], ACT.Sqrt).then_inc(a0, 1)
            act.wait_ge(d0, D_HPRE)
            nc.scalar.activation(hc_[:], ae[:], ACT.Gelu).then_inc(a0, 1)
            act.wait_ge(small_in, 16 * 7)
            nc.scalar.copy(rwhl[:, :, 0:E], rwr[:, 0:KC, :]).then_inc(a0, 1)
            for i in range(PIECES):
                act.wait_ge(wraw_in[i % 2], 16 * (i // 2 + 1))
                nc.scalar.copy(piece_of(w13h, w2h, i), wraw[:, i % 2]).then_inc(wsh, 1)

            def cut_stack(b):
                act.wait_ge(stk_in, b * 48 + 48)
                if not first(b):
                    act.wait_ge(lay_ps, b * KC)
                nc.scalar.copy(stk[:], stkr[:]).then_inc(stk_hi, 1)

            def cut_xt(b, c):
                act.wait_ge(xt_ps, b * KC + c + 1)
                nc.scalar.copy(xTh[:, c], K[c % 2][:]).then_inc(xt_hi, 1)

            def cut_layer(b, c):
                act.wait_ge(lay_f, b * KC + c + 1)
                nc.scalar.copy(layh[:, c], layf[:, c % 2]).then_inc(lay_hi, 1)

            def exp_scores(b):
                act.wait_ge(z_sb, b + 1)
                nc.scalar.activation(rs[1][:, :, 0], rs[0][:, :, 0], ACT.Exp, scale=-1.0).then_inc(ez, 1)

            def keep_tok(b, slot, t):
                act.wait_ge(tok_ps, b * TT + t + 1)
                nc.scalar.copy(x1tok[:, slot, t], K[t % 2][:]).then_inc(tok_sb, 1)

            act.wait_ge(xw_ps, NCH)
            act.wait_ge(wsh, PIECES)
            act.wait_ge(wsl, PIECES)
            cut_stack(0)
            act.wait_ge(xw_sb, NCH)
            for c in range(2):
                cut_xt(0, c)
                cut_layer(0, c)

            def body(b, slot):
                cut_xt(b, 2)
                cut_layer(b, 2)
                if not first(b):
                    keep_tok(b - 1, 1 - slot, 2)
                    keep_tok(b - 1, 1 - slot, 3)
                cut_xt(b, 3)
                cut_layer(b, 3)
                if not last(b):
                    cut_stack(b + 1)
                if not first(b):
                    exp_scores(b - 1)
                    act.wait_ge(x1T_out, b * 16)
                    act.wait_ge(x1_lo, b * KC)
                if not last(b):
                    cut_xt(b + 1, 0)
                for c in range(KC):
                    act.wait_ge(main_ps, b * KC + c + 1)
                    nc.scalar.copy(x1T[:, c], M[c][:]).then_inc(x1_f, 1)
                if not last(b):
                    cut_layer(b + 1, 0)
                    cut_xt(b + 1, 1)
                    cut_layer(b + 1, 1)
                wait_slot(b, slot)
                for c in range(KC):
                    if c >= 2:
                        keep_tok(b, slot, c - 2)
                    if c == 0:
                        act.wait_ge(x1_f, b * KC + KC)
                    nc.scalar.copy(x1h[:, c], x1T[:, c]).then_inc(x1_hi, 1)

            def wait_slot(b, slot):
                half = (b - slot) >> 1
                if isinstance(b, int) and half == 0:
                    return
                act.wait_ge(scat[slot], half * (16 * TT * TOPK))
                act.wait_ge(x1_out[slot], half * 16)

            def done():
                keep_tok(NB - 1, 1, 2)
                keep_tok(NB - 1, 1, 3)
                exp_scores(NB - 1)

            blocks(act, body, done)
            ffn_act(act, S, 0, True)
            def cut_x(n):
                act.wait_ge(xg_ps, n)
                nc.scalar.copy(xgh[:].rearrange("p k n -> p (k n)"), TX[:]).then_inc(xg_hi, 1)

            def gelu(n):
                act.wait_ge(h_ps, n)
                nc.scalar.activation(hg[:], HP[:], ACT.Gelu).then_inc(h_g, 1)

            def cut_h(n):
                act.wait_ge(ht_ps, n)
                nc.scalar.copy(hTh[:].rearrange("p k n -> p (k n)"), TH[:]).then_inc(ht_hi, 1)

            act.wait_ge(S.g_lo, HC)
            act.wait_ge(tab_in, 16)
            cut_x(1)
            gelu(1)
            cut_x(2)
            cut_h(1)
            pairs = value(act, PAIRS, 0, PAIRS_MAX, 1)

            def rpair(j):
                for s in range(2):
                    t = j * 2 + s
                    gelu(t + 2)
                    cut_x(t + 3)
                    cut_h(t + 2)
            tiles(act, pairs, rpair)
            for s in range(2):
                act.wait_ge(y_out[s], pairs * 16)
            act.wait_ge(ht_lo, pairs * 2 + 1)
            act.wait_ge(xg_lo, pairs * 2 + 2)

            def fblock(b):
                act.wait_ge(x1raw_in, b * 16 + 16)
                if not first(b):
                    act.wait_ge(F.v_ps, b * HC)
                for c in range(KC):
                    nc.scalar.copy(x1h[:, c], x1raw[:, c * T:(c + 1) * T]).then_inc(xf_hi, 1)
                ffn_act(act, F, b, first(b))
            fblock(0)
            with act.Fori(1, NB - 1) as b:
                fblock(b)

        def tables(dve):
            n = [0]

            def link(ins):
                n[0] += 1
                ins.then_inc(dt_, 1)
                dve.wait_ge(dt_, n[0])

            tt, ts, red = nc.vector.tensor_tensor, nc.vector.tensor_scalar, nc.vector.tensor_reduce
            cnt, nt, active, ends, ranks, past, rows, t7, t8, t9 = (tw[:, i] for i in range(10))
            col = [tab[:, i:i + 1] for i in range(8)]
            tmp = [tw[:, 10, i:i + 1] for i in range(4)]
            ti = [twi[:, 1, i:i + 1] for i in range(4)]
            link(nc.vector.scalar_tensor_tensor(out=cnt, in0=iota8[:], scalar=-float(REGION), in1=run[:, TT],
                                                op0=ALU.mult, op1=ALU.add))
            link(ts(twi[:, 0], cnt, float(P - 1), None, ALU.add))
            link(ts(twi[:, 0], twi[:, 0], 7, None, ALU.logical_shift_right))
            link(nc.vector.tensor_copy(nt, twi[:, 0]))
            link(ts(active, nt, 0.0, None, ALU.is_gt))
            link(nc.vector.tensor_tensor_scan(ends, ones[:, 0:E], nt, 0.0, ALU.mult, ALU.add))
            link(nc.vector.tensor_tensor_scan(ranks, ones[:, 0:E], active, 0.0, ALU.mult, ALU.add))
            link(ts(past, ends, iotap[:, 0:1], None, ALU.is_le))
            link(ts(rows, nt, -float(P), float(REGION), ALU.mult, ALU.add))
            link(tt(rows, rows, past, ALU.mult))
            link(red(tmp[0], rows, AX, ALU.add))
            link(nc.vector.scalar_tensor_tensor(out=tmp[0], in0=iotap[:], scalar=float(P), in1=tmp[0],
                                                op0=ALU.mult, op1=ALU.add))
            link(ts(col[ROW], tmp[0], float(E * REGION), None, ALU.min))
            link(tt(t7, active, past, ALU.mult))
            link(red(tmp[1], t7, AX, ALU.add))
            link(nc.vector.tensor_copy(col[NACT], ranks[:, E - 1:E]))
            link(ts(tmp[2], col[NACT], -1.0, None, ALU.add))
            link(tt(tmp[1], tmp[1], tmp[2], ALU.min))
            link(ts(col[WCNT], tmp[1], 2.0, 1.0, ALU.mult, ALU.add))
            link(nc.vector.tensor_copy(ti[0], tmp[1]))
            link(ts(ti[0], ti[0], 1, None, ALU.bitwise_and))
            link(nc.vector.tensor_copy(tmp[1], ti[0]))
            link(ts(col[WOFF], tmp[1], float(WSL), None, ALU.mult))
            link(ts(t7, ranks, iotap[:, 0:1], None, ALU.is_le))
            link(red(tmp[3], t7, AX, ALU.add))
            link(ts(col[AROW], tmp[3], float(E - 1), float(KC), ALU.min, ALU.mult))
            link(ts(t8, ranks, iotap[:, 0:1], None, ALU.is_lt))
            link(tt(t8, t8, nt, ALU.mult))
            link(red(col[FREE], t8, AX, ALU.add))
            link(tt(t9, ident[:, 0:E], run[:, TT], ALU.mult))
            link(red(col[PAD], t9, AX, ALU.add))
            link(ts(ti[1], ends[:, E - 1:E], 1.0, None, ALU.add))
            link(ts(ti[1], ti[1], 1, None, ALU.logical_shift_right))
            link(nc.vector.tensor_copy(col[PAIRS], ti[1]))
            nc.vector.tensor_copy(tabi[:], tab[:]).then_inc(tabs, 1)
            link(ts(t9, nt, float(P), -float(REGION), ALU.mult, ALU.add))
            link(nc.vector.tensor_copy(slots[:], pos_all[:]))
            for e in range(1, E):
                link(ts(step[:], pos_all[:], float(e * REGION), t9[:, e - 1:e], ALU.is_ge, ALU.mult))
                link(tt(slots[:], slots[:], step[:], ALU.add))
            nc.vector.tensor_copy(ypos[:], slots[:]).then_inc(tabs, 1)

        @block.vector
        def _(dve):
            tt, ts = nc.vector.tensor_tensor, nc.vector.tensor_scalar
            n0 = [0]

            def link(ins):
                n0[0] += 1
                ins.then_inc(d0, 1)
                dve.wait_ge(d0, n0[0])

            dve.wait_ge(small_in, 16 * 7)
            link(nc.vector.bn_stats(stats[:, 0:6], craw[:]))
            link(nc.vector.bn_aggr(stats[:, 6:8], stats[:, 0:6]))
            link(ts(stats[:, 8:9], stats[:, 7:8], LN_EPS, None, ALU.add))
            assert n0[0] == D_VAR
            dve.wait_ge(a0, 1)
            link(nc.vector.reciprocal(stats[:, 10:11], stats[:, 9:10]))
            link(ts(ae[:], craw[:], stats[:, 6:7], stats[:, 10:11], ALU.subtract, ALU.mult))
            link(tt(ae[:], ae[:], lng[:], ALU.mult))
            link(tt(ae[:], ae[:], lnb[:], ALU.add))
            assert n0[0] == D_AE
            dve.wait_ge(p0, 1)
            link(nc.vector.tensor_copy(actT[:, 0].rearrange("p k b -> p (k b)"), K[0][:, 0:KC * 8]))
            dve.wait_ge(p0, 2)
            link(nc.vector.tensor_copy(actT[:, 1].rearrange("p k b -> p (k b)"), K[1][:, 0:KC * 8]))
            dve.wait_ge(p0, 3)
            link(tt(ae[:], L[0:8, :], cb1b[:], ALU.add))
            assert n0[0] == D_HPRE
            dve.wait_ge(p0, 4)
            link(nc.vector.tensor_copy(actT[:, 2].rearrange("p k b -> p (k b)"), K[0][:, 0:KC * 8]))
            assert n0[0] == D_HT
            dve.wait_ge(a0, 3)
            link(tt(rwhl[:, :, E:2 * E], rwr[:, 0:KC, :], rwhl[:, :, 0:E].bitcast(F32), ALU.subtract))
            dve.wait_ge(p0, 5)
            link(nc.vector.tensor_copy(stats[:, 8:16], Rb[0:8, 0:E]))
            dve.wait_ge(consts, 7)
            link(tt(tbs[:], ident[0:8, 0:NB].unsqueeze(2).broadcast_to([8, NB, E]),
                    stats[:, 8:16].unsqueeze(1).broadcast_to([8, NB, E]), ALU.mult))
            assert n0[0] == D_TBS
            dve.wait_ge(p0, 6)
            link(nc.vector.tensor_copy(tb[:].rearrange("p b e -> p (b e)"), Rb[:, 64:64 + NB * E]))
            assert n0[0] == D_TB
            piece = 0

            def cut_piece(i):
                dve.wait_ge(wsh, i + 1)
                tt(piece_of(w13l, w2l, i), wraw[:, i % 2], piece_of(w13h, w2h, i).bitcast(F32),
                   ALU.subtract).then_inc(wsl, 1)
            for n in range(NCH):
                dve.wait_ge(xw_ps, n + 1)
                if n >= 2:
                    dve.wait_ge(xwc_out[n % 2], 16 * (n // 2))
                tt(xwc[:, n % 2].rearrange("b r w -> b w r"),
                   M[n % 2][0:8, :].rearrange("b (w r) -> b w r", r=RK),
                   b2c[:, n % RING].rearrange("b (w r) -> b w r", r=RK), ALU.add).then_inc(xw_sb, 1)
                if n >= 6 and n % 2 == 0 and piece < PIECES:
                    cut_piece(piece)
                    piece += 1
            while piece < PIECES:
                cut_piece(piece)
                piece += 1
            dve.wait_ge(base_in, 16)
            for c in range(KC):
                v = basep[:, c, c * P:(c + 1) * P]
                last_ins = nc.vector.scalar_tensor_tensor(out=v, in0=ident[:], scalar=2.0, in1=v,
                                                          op0=ALU.mult, op1=ALU.add).then_inc(dr, 1)
            ts(run[:, TT], iota8[:], float(REGION), None, ALU.mult).then_inc(dr, 1)
            dve.wait_ge(dr, 5)
            DR0 = 5
            dve.wait_ge(wsl, PIECES)

            def cut_xt(b, c):
                dve.wait_ge(xt_hi, b * KC + c + 1)
                tt(xTl[:, c], K[c % 2][:], xTh[:, c].bitcast(F32), ALU.subtract).then_inc(xt_lo, 1)

            def layer(b, c):
                dve.wait_ge(lay_ps, b * KC + c + 1)
                tt(layf[:, c % 2], L[:], basep[:, c], ALU.add).then_inc(lay_f, 1)
                dve.wait_ge(lay_hi, b * KC + c + 1)
                tt(layl[:, c], layf[:, c % 2], layh[:, c].bitcast(F32), ALU.subtract).then_inc(lay_lo, 1)

            PLACES = 7
            CHAIN = 15 + 2 * TT + PLACES

            def scores(b):
                k = [0]

                def step(ins):
                    k[0] += 1
                    ins.then_inc(dr, 1)

                def link(ins):
                    step(ins)
                    dve.wait_ge(dr, b * CHAIN + (DR0 + k[0]))

                z, e_, s = rs[0][:, :, 0], rs[1][:, :, 0], rs[2][:, :, 0]
                zp = Rb[:, 0:TT * 2 * E].rearrange("p (t e) -> p t e", t=TT)
                dve.wait_ge(z_ps, b + 1)
                link(tt(z, zp[:, :, 0:E], tb[:, ds(b, 1), :].broadcast_to([P, TT, E]), ALU.add))
                tt(z, zp[:, :, E:2 * E], z, ALU.add).then_inc(z_sb, 1)
                dve.wait_ge(ez, b + 1)
                link(ts(e_, e_, 1.0, None, ALU.add))
                link(nc.vector.reciprocal(s, e_))
                link(tt(z, s, rbias[:].unsqueeze(1).broadcast_to([P, TT, E]), ALU.add))
                alone(dve)
                for t in range(TT):
                    (step if t < TT - 1 else link)(nc.vector.max(mx[:, t], z[:, t]))
                alone(dve)
                for t in range(TT):
                    (step if t < TT - 1 else link)(nc.vector.max_index(mi[:, t], mx[:, t], z[:, t]))
                link(nc.vector.tensor_copy(mx[:], mi[:]))
                link(tt(msk[:], iota8[:].unsqueeze(1).unsqueeze(1).broadcast_to([P, TT, TOPK, E]),
                        mx[:, :, 0:TOPK].unsqueeze(3).broadcast_to([P, TT, TOPK, E]), ALU.is_equal))
                tt(mx[:], msk[:, :, 0], msk[:, :, 1], ALU.add).then_inc(masks, 1)
                link(tt(rs[3][:], msk[:], s.unsqueeze(2).broadcast_to([P, TT, TOPK, E]), ALU.mult))
                sel = sg[0][:, 0:TT * TOPK].rearrange("p (t k) -> p t k", k=TOPK)
                link(nc.vector.tensor_reduce(sel, rs[3][:], AX, ALU.add))
                den, c, h, r = (sg[1][:, i * TT:(i + 1) * TT] for i in range(4))
                link(tt(den, sel[:, :, 0], sel[:, :, 1], ALU.add))
                step(ts(r, den, GATE_EPS, None, ALU.add))
                link(ts(c, den, GATE_EPS, None, ALU.is_gt))
                step(nc.vector.reciprocal(r, r))
                link(ts(h, c, -0.5 / 3, 0.5 / 3, ALU.mult, ALU.add))
                link(nc.vector.scalar_tensor_tensor(out=r, in0=r, scalar=1.0 / 3, in1=c, op0=ALU.mult, op1=ALU.mult))
                g2 = sg[2][:, 0:TT * TOPK].rearrange("p (t k) -> p t k", k=TOPK)
                link(tt(g2, sel, r.unsqueeze(2).broadcast_to([P, TT, TOPK]), ALU.mult))
                gall = gate_all[:, ds(b * (TT * TOPK), TT * TOPK)].rearrange("p (t k) -> p t k", k=TOPK)
                tt(gall, g2, h.unsqueeze(2).broadcast_to([P, TT, TOPK]), ALU.add).then_inc(gates, 1)
                assert k[0] == CHAIN - PLACES, k[0]

            def places(b, slot):
                k = [CHAIN - PLACES]

                def link(ins):
                    k[0] += 1
                    ins.then_inc(dr, 1)
                    dve.wait_ge(dr, b * CHAIN + (DR0 + k[0]))

                dve.wait_ge(rank_ps, b + 1)
                pre_ps = Rb[:, 64:64 + TT * E].rearrange("p (t e) -> p t e", t=TT)
                tot_ps = Rb[:, 96:96 + TT * E].rearrange("p (t e) -> p t e", t=TT)
                link(nc.vector.tensor_copy(run[:, 0], run[:, TT]))
                for t in range(TT):
                    link(tt(run[:, t + 1], run[:, t], tot_ps[:, t], ALU.add))
                link(tt(mx[:], pre_ps, run[:, 0:TT], ALU.add))
                link(tt(rs[3][:], msk[:], mx[:].unsqueeze(2).broadcast_to([P, TT, TOPK, E]), ALU.mult))
                pf = sg[0][:, 0:TT * TOPK].rearrange("p (t k) -> p t k", k=TOPK)
                nc.vector.tensor_reduce(pf, rs[3][:], AX, ALU.add).then_inc(masks, 1)
                assert k[0] == CHAIN, k[0]

            def store_places(b, slot):
                dve.wait_ge(masks, b * 2 + 2)
                nc.vector.tensor_copy(pos_all[:, ds(b * (TT * TOPK), TT * TOPK)], sg[0][:, 0:TT * TOPK]).then_inc(places_all, 1)
                half = (b - slot) >> 1
                if not isinstance(b, int) or half > 0:
                    dve.wait_ge(scat[slot], half * (16 * TT * TOPK))
                nc.vector.tensor_copy(pos_fix[:, slot], sg[0][:, 0:TT * TOPK]).then_inc(pos_rdy, 1)

            def cut_stack(b):
                dve.wait_ge(stk_hi, b + 1)
                for a, g in ((0, GROUPS[1]), (1, GROUPS[2])):
                    s = stk[g:g + RK, a]
                    tt(s, stkr[g:g + RK, a], s.bitcast(F32), ALU.subtract).then_inc(stk_lo, 1)

            cut_stack(0)
            for c in range(2):
                cut_xt(0, c)
                layer(0, c)

            def body(b, slot):
                for c in (2, 3):
                    cut_xt(b, c)
                    layer(b, c)
                if not last(b):
                    cut_stack(b + 1)
                if not first(b):
                    scores(b - 1)
                if not last(b):
                    cut_xt(b + 1, 0)
                    layer(b + 1, 0)
                    cut_xt(b + 1, 1)
                    layer(b + 1, 1)
                if not first(b):
                    places(b - 1, 1 - slot)
                    store_places(b - 1, 1 - slot)

            def done():
                scores(NB - 1)
                places(NB - 1, 1)
                store_places(NB - 1, 1)
                dve.wait_ge(places_all, NB)
                dve.wait_ge(gates, NB)

            blocks(dve, body, done)
            tables(dve)
            ffn_dve(dve, S, 0)

            def cut_x(n):
                dve.wait_ge(xg_hi, n)
                tt(xgl[:].rearrange("p k n -> p (k n)"), TX[:],
                   xgh[:].rearrange("p k n -> p (k n)").bitcast(F32), ALU.subtract).then_inc(xg_lo, 1)

            def cut_h(n):
                dve.wait_ge(ht_hi, n)
                tt(hTl[:].rearrange("p k n -> p (k n)"), TH[:],
                   hTh[:].rearrange("p k n -> p (k n)").bitcast(F32), ALU.subtract).then_inc(ht_lo, 1)

            dve.wait_ge(tab_in, 16)
            cut_x(1)
            cut_x(2)
            cut_h(1)
            pairs = value(dve, PAIRS, 0, PAIRS_MAX, 1)

            def rpair(j):
                for s in range(2):
                    t = j * 2 + s
                    cut_x(t + 3)
                    dve.wait_ge(y_ps, t + 2)
                    if not first(j):
                        dve.wait_ge(y_out[s], j * 16)
                    nc.vector.tensor_copy(yo[:, s], YP[:]).then_inc(y_sb, 1)
                    cut_h(t + 2)
            tiles(dve, pairs, rpair)

            def combine(b, m):
                nc.vector.tensor_copy(gate_fix[:], gate_all[:, ds(b * (TT * TOPK), TT * TOPK)]).then_inc(gate_f, 1)
                dve.wait_ge(gate_f, m + 1)
                dve.wait_ge(xres_in, m * 16 + 16)
                for t in range(TT):
                    if isinstance(m, int) and m == 0:
                        dve.wait_ge(S.sum_ps, t + 1)
                    else:
                        dve.wait_ge(F.sum_ps, b * TT + (t + 1))
                    nc.vector.scalar_tensor_tensor(out=xres[:, t], in0=M[t][:], scalar=1.0 / 3, in1=xres[:, t],
                                                   op0=ALU.mult, op1=ALU.add).then_inc(acc, 1)
                dve.wait_ge(y_in, m * (16 * TT * TOPK) + 16 * TT * TOPK)
                for k in range(TOPK):
                    for t in range(TT):
                        dve.wait_ge(acc, m * (2 * TT) + (k * TT + t + 1))
                        c = t * TOPK + k
                        nc.vector.scalar_tensor_tensor(
                            out=xres[:, t], in0=yb[:, c], scalar=gate_fix[:, c:c + 1], in1=xres[:, t],
                            op0=ALU.mult, op1=ALU.add).then_inc(acc if k == 0 else comb, 1)

            def cut_block(b):
                for c in range(KC):
                    dve.wait_ge(xf_hi, b * KC + c + 1)
                    tt(x1l[:, c], x1raw[:, c * T:(c + 1) * T], x1h[:, c].bitcast(F32),
                       ALU.subtract).then_inc(xf_lo, 1)

            cut_block(0)
            combine(NB - 1, 0)
            with dve.Fori(0, NB - 2) as b:
                ffn_dve(dve, F, b)
                cut_block(b + 1)
                combine(b, b + 1)
            ffn_dve(dve, F, NB - 2)
            combine(NB - 2, NB - 1)

        @block.tensor
        def _(pe):
            mm = nc.tensor.matmul

            def mm3(o, ah, al, bh, bl, start, stop):
                mm(o, ah, bh, start=start, stop=False)
                mm(o, ah, bl, start=False, stop=False)
                return mm(o, al, bh, start=False, stop=stop)

            def turn8(dst, src, k):
                return nc.tensor.transpose(dst[:, k * 8:(k + 1) * 8], src[:, k * P:(k + 1) * P], ident[0:8, 0:8])

            pe.wait_ge(consts, 3)
            pe.wait_ge(small_in, 16 * 7)
            for k in range(KC):
                last_mm = turn8(K[0], craw, k)
            last_mm.then_inc(p0, 1)
            pe.wait_ge(d0, D_AE)
            for k in range(KC):
                last_mm = turn8(K[1], ae, k)
            last_mm.then_inc(p0, 1)
            pe.wait_ge(d0, D_AET)
            for k in range(KC):
                last_mm = mm(L[0:8, :], actT[:, 1, k], w1c[:, k], start=(k == 0), stop=(k == KC - 1))
            last_mm.then_inc(p0, 1)
            pe.wait_ge(a0, 2)
            for k in range(KC):
                last_mm = turn8(K[0], hc_, k)
            last_mm.then_inc(p0, 1)
            for k in range(KC):
                last_mm = mm(Rb[0:8, 0:E], actT[:, 0, k], rwr[:, KC + k], start=(k == 0), stop=(k == KC - 1))
            last_mm.then_inc(p0, 1)
            pe.wait_ge(d0, D_TBS)
            mm(Rb[:, 64:64 + NB * E], ones[0:8, :], tbs[:].rearrange("p b e -> p (b e)"),
               start=True, stop=True).then_inc(p0, 1)
            for n in range(NCH):
                pe.wait_ge(w2c_in[n % RING], 32 * (n // RING + 1))
                if n >= 2:
                    pe.wait_ge(xw_sb, n - 1)
                for k in range(KC):
                    last_mm = mm(M[n % 2][0:8, :], actT[:, 2, k], w2c[:, n % RING, k],
                                 start=(k == 0), stop=(k == KC - 1))
                last_mm.then_inc(xw_ps, 1)

            def xtr(b, c):
                pe.wait_ge(x_in[c], b * 16 + 16)
                if c == 0 and not first(b):
                    if isinstance(b, int) and b == 1:
                        pe.wait_ge(xt_lo, 3)
                    else:
                        pe.wait_ge(tok_sb, b * TT - 5)
                elif c == 1 and not first(b):
                    pe.wait_ge(xt_lo, b * KC)
                elif c >= 2 and first(b):
                    pe.wait_ge(xt_lo, c - 1)
                elif c == 2:
                    pe.wait_ge(tok_sb, b * TT - 3)
                elif c == 3:
                    pe.wait_ge(tok_sb, b * TT)
                for t in range(TT):
                    last_mm = nc.tensor.transpose(K[c % 2][:, t * P:(t + 1) * P], xtok[:, t, c * P:(c + 1) * P], ident[:])
                last_mm.then_inc(xt_ps, 1)

            def lay(b, c):
                pe.wait_ge(stk_lo, b * 2 + 2)
                if c > 0 or not first(b):
                    pe.wait_ge(lay_f, b * KC + c)
                mm(L[:], stk[:, 0, c * P:(c + 1) * P], stk[:, 1], start=True, stop=True).then_inc(lay_ps, 1)

            def main(b, c):
                pe.wait_ge(xt_lo, b * KC + c + 1)
                pe.wait_ge(lay_lo, b * KC + c + 1)
                for o in range(KC):
                    if c == 0 and not first(b):
                        pe.wait_ge(x1_f, b * KC + (o - 3))
                    cols = slice(o * P, (o + 1) * P)
                    last_mm = mm3(M[o][:], layh[:, c, cols], layl[:, c, cols], xTh[:, c], xTl[:, c], c == 0, c == KC - 1)
                    if c == KC - 1:
                        last_mm.then_inc(main_ps, 1)

            def tok(b, t):
                pe.wait_ge(x1_f, b * KC + KC)
                if t == 0:
                    pe.wait_ge(*((tok_sb, b * TT - 1) if last(b) else (xt_lo, b * KC + 5)))
                elif t == 1:
                    pe.wait_ge(xt_lo, b * KC + (4 if last(b) else 6))
                elif t == 2:
                    pe.wait_ge(*((tok_sb, b * TT + 1) if last(b) else (xt_lo, b * KC + 7)))
                else:
                    pe.wait_ge(tok_sb, b * TT + 2)
                for o in range(KC):
                    last_mm = nc.tensor.transpose(K[t % 2][:, o * P:(o + 1) * P], x1T[:, o, t * P:(t + 1) * P], ident[:])
                last_mm.then_inc(tok_ps, 1)

            def router(b):
                pe.wait_ge(x1_lo, b * KC + KC)
                if not first(b):
                    pe.wait_ge(pos_rdy, b)
                for t in range(TT):
                    rows = slice(t * P, (t + 1) * P)
                    for k in range(KC):
                        mm(Rb[:, t * 16:t * 16 + 2 * E], x1h[:, k, rows], rwhl[:, k], start=(k == 0), stop=False)
                        last_mm = mm(Rb[:, t * 16:t * 16 + E], x1l[:, k, rows], rwhl[:, k, 0:E],
                                     start=False, stop=(k == KC - 1))
                last_mm.then_inc(z_ps, 1)

            def rank(b):
                pe.wait_ge(masks, b * 2 + 1)
                m = mx[:].rearrange("p t e -> p (t e)")
                mm(Rb[:, 64:64 + TT * E], upper[:], m, start=True, stop=True)
                mm(Rb[:, 96:96 + TT * E], ones[:], m, start=True, stop=True).then_inc(rank_ps, 1)

            for c in range(2):
                xtr(0, c)
                lay(0, c)

            def body(b, slot):
                main(b, 0)
                xtr(b, 2)
                lay(b, 2)
                if not first(b):
                    tok(b - 1, 2)
                    tok(b - 1, 3)
                main(b, 1)
                xtr(b, 3)
                lay(b, 3)
                if not first(b):
                    router(b - 1)
                main(b, 2)
                if not last(b):
                    xtr(b + 1, 0)
                main(b, 3)
                if not last(b):
                    lay(b + 1, 0)
                    xtr(b + 1, 1)
                    lay(b + 1, 1)
                tok(b, 0)
                tok(b, 1)
                if not first(b):
                    rank(b - 1)

            def done():
                tok(NB - 1, 2)
                tok(NB - 1, 3)
                router(NB - 1)

            blocks(pe, body, done)

            def ffn(S, b, banks, x_ready, between, sum_free):
                def sums(h):
                    pe.wait_ge(S.g_lo, b * HC + h + 1)
                    for t in range(TT):
                        if h == 0:
                            sum_free(t)
                        rows = slice(t * P, (t + 1) * P)
                        s_ = h % 2
                        last_mm = mm3(M[t][:], gTh[:, s_, rows], gTl[:, s_, rows], w2h[:, h], w2l[:, h], h == 0, h == HC - 1)
                        if h == HC - 1:
                            last_mm.then_inc(S.sum_ps, 1)
                    if h < HC - 1:
                        last_mm.then_inc(S.o_ps, 1)

                for h in range(HC):
                    n = b * HC + h
                    if h < 2 and banks is not None:
                        banks(h)
                    else:
                        pe.wait_ge(S.silu, n - 1)
                        pe.wait_ge(S.g_f, n - 1)
                    cols = slice(h * P, (h + 1) * P)
                    for i, (bank, s_) in enumerate(((U[h % 2], S.u_ps), (V[h % 2], S.v_ps))):
                        for k in range(KC):
                            if h == 0 and i == 0:
                                x_ready(k)
                            last_mm = mm3(bank[:], w13h[:, i, k, cols], w13l[:, i, k, cols], x1h[:, k], x1l[:, k],
                                          k == 0, k == KC - 1)
                        last_mm.then_inc(s_, 1)
                    if h == 0:
                        between()
                    else:
                        sums(h - 1)
                sums(HC - 1)

            def banks_s(h):
                pe.wait_ge(tok_sb, NB * TT)
                pe.wait_ge(lay_f, NB * KC)
                if h == 1:
                    pe.wait_ge(pos_rdy, NB)
            ffn(S, 0, banks_s, lambda k: pe.wait_ge(x1_lo, NB * KC), lambda: rank(NB - 1),
                lambda t: pe.wait_ge(x1_hi, NB * KC))

            pe.sem_inc(y_ps, 1)
            pe.wait_ge(tab_in, 16)
            pe.wait_ge(S.silu, HC)
            pe.wait_ge(S.g_f, HC)

            def tx(t, slot):
                pe.wait_ge(xr_in[slot], ((t - slot) >> 1) * 16 + 16)
                pe.wait_ge(xg_lo, t)
                for k in range(KC):
                    last_mm = nc.tensor.transpose(TX[:, k * P:(k + 1) * P], xr[:, slot, k * P:(k + 1) * P], ident[:])
                last_mm.then_inc(xg_ps, 1)

            def expert(t, m, o, ah, al, ready, free, done_):
                off = value(pe, WOFF, t, WSL)
                need = value(pe, WCNT, t, 2 * E, 1)
                pe.wait_ge(we_lo, need + m)
                ready()
                free()
                for k in range(KC):
                    last_mm = mm3(o, ah[:, k], al[:, k], weh[:, m, ds(off + k * HE, HE)], wel[:, m, ds(off + k * HE, HE)],
                                  k == 0, k == KC - 1)
                last_mm.then_inc(done_, 1)

            def mm1(t):
                expert(t, 0, HP[:], xgh, xgl, lambda: pe.wait_ge(xg_lo, t + 1), lambda: pe.wait_ge(h_g, t), h_ps)

            def mm2(t):
                expert(t, 1, YP[:], hTh, hTl, lambda: pe.wait_ge(ht_lo, t + 1), lambda: pe.wait_ge(y_sb, t), y_ps)

            def th(t):
                pe.wait_ge(h_g, t + 1)
                pe.wait_ge(ht_lo, t)
                for k in range(KC):
                    last_mm = nc.tensor.transpose(TH[:, k * P:(k + 1) * P], hg[:, k * P:(k + 1) * P], ident[:])
                last_mm.then_inc(ht_ps, 1)

            tx(0, 0)
            mm1(0)
            tx(1, 1)
            th(0)
            pairs = value(pe, PAIRS, 0, PAIRS_MAX, 1)

            def rpair(j):
                for s in range(2):
                    t = j * 2 + s
                    mm1(t + 1)
                    tx(t + 2, s)
                    mm2(t)
                    th(t + 1)
            tiles(pe, pairs, rpair)

            pe.wait_ge(xg_lo, pairs * 2 + 2)
            pe.wait_ge(ht_lo, pairs * 2 + 1)
            pe.wait_ge(h_g, pairs * 2 + 1)
            pe.wait_ge(y_sb, pairs * 2)

            def fblock(b):
                ffn(F, b, (lambda h: None) if first(b) else None, lambda k: pe.wait_ge(xf_lo, b * KC + k + 1),
                    lambda: None, lambda t: pe.wait_ge(acc, b * (2 * TT) + t + 1))
            fblock(0)
            with pe.Fori(1, NB - 1) as b:
                fblock(b)


_INS = ['x', 'cond_1024', 'L0_cond_base_layer', 'L0_cond_w1', 'L0_cond_b1', 'L0_cond_w2', 'L0_cond_b2', 'L0_cond_ln_g',
        'L0_cond_ln_b', 'L1_cond_router_W', 'L1_cond_router_bias', 'L1_cond_w1', 'L1_cond_w3', 'L1_cond_w2',
        'L1_cond_W1e', 'L1_cond_W2e']
_OUTS = [((8, 512, 512), 'float32')]


def kernel(**inputs):
    import numpy as _np
    import concourse.bacc as _bacc
    from concourse import mybir as _mybir
    from concourse.bass_utils import run_bass_kernel_spmd as _run

    nc = _bacc.Bacc("TRN2", target_bir_lowering=False, num_devices=1)
    arrays, args = {}, []
    for name in _INS:
        a = _np.ascontiguousarray(inputs[name])
        arrays[f"in_{name}_dram"] = a
        args.append(nc.dram_tensor(f"in_{name}_dram", a.shape, _mybir.dt.from_np(a.dtype), kind="ExternalInput").ap())
    for i, (shape, dtype) in enumerate(_OUTS):
        dt = _mybir.dt.from_np(_np.dtype(dtype))
        args.append(nc.dram_tensor(f"out_{i}_dram", shape, dt, kind="ExternalOutput").ap())
    build(nc, *args)
    r = _run(nc, [arrays], core_ids=[0])
    got = tuple(r.results[0][f"out_{i}_dram"] for i in range(len(_OUTS)))
    return got[0]
```

```python
from contextlib import ExitStack

import concourse.bass as bass
from concourse import mybir

ALU = mybir.AluOpType
ACT = mybir.ActivationFunctionType
F32 = mybir.dt.float32
F32R = mybir.dt.float32r
I32 = mybir.dt.int32
U32 = mybir.dt.uint32
AX = mybir.AxisListType.X
ds = bass.ds

P = 128
TOPK = 2
LN_EPS = 1e-5
GATE_EPS = 1e-9
CH = 512
RING = 4
GROUPS = (0, 32, 64)
ROW, WOFF, WCNT, AROW, FREE, PAD, PAIRS, NACT = range(8)


def build(nc, x, cond, base, cw1, cb1, cw2, cb2, ln_g, ln_b, rw, rb, w1, w3, w2, w1e, w2e, out):
    NB, T, D = x.shape
    KC = D // P
    TT = T // P
    HS = w1.shape[1]
    HC = HS // P
    E, _, HE = w1e.shape
    RK = cw2.shape[1] // (2 * D)
    N = NB * T
    NT = N // P
    REGION = N + P
    ROWS = E * REGION + P
    STACK = GROUPS[-1] + RK
    NCH = cw2.shape[1] // CH
    WPC = CH // RK
    WSL = KC * HE
    PIECE = HS
    PIECES = (2 * KC * HS + HC * D) // PIECE
    TILES = (N * TOPK + E * (P - 1)) // P
    PAIRS_MAX = (TILES + 1) // 2
    TAB = -(-(TILES + 5) // 8) * 8
    assert NB == 8 and T == D == HE == CH and TT == KC == 4 and E == 8 and HS == 1024 and RK == 8

    xw_d = nc.dram_tensor("xw_d", (NB, 2, RK, D), F32, kind="Internal").ap()
    x1_d = nc.dram_tensor("x1_d", (N, D), F32, kind="Internal").ap()
    x1T_d = nc.dram_tensor("x1T_d", (P, NB, KC * T), F32, kind="Internal").ap()
    xs_d = nc.dram_tensor("xs_d", (ROWS, D), F32, kind="Internal").ap()
    tab_d = nc.dram_tensor("tab_d", (TAB, 8), I32, kind="Internal").ap()
    ys_d = nc.dram_tensor("ys_d", (PAIRS_MAX * 2 * P, D), F32, kind="Internal").ap()

    x_view = x.rearrange("b (t p) d -> p (b t) d", p=P)
    out_view = out.rearrange("b (t p) d -> p (b t) d", p=P)
    x1_view = x1_d.rearrange("(n p) d -> p n d", p=P)
    w1e_view = w1e.rearrange("e (k p) n -> p (e k) n", p=P)
    w2e_view = w2e.rearrange("e (k p) n -> p (e k) n", p=P)
    cw2_view = cw2.rearrange("(k p) n -> p k n", p=P)

    def row_bc(v, parts):
        return v.rearrange("(a n) -> a n", a=1).broadcast_to([parts, v.shape[0]])

    with ExitStack() as ctx:
        def sb(name, shape, dt=F32, where=ctx):
            return where.enter_context(nc.sbuf_tensor(name, shape, dt))

        def sem(name):
            return ctx.enter_context(nc.semaphore(name))

        M = [ctx.enter_context(nc.psum_tensor(f"M{i}", [P, CH], F32)) for i in range(4)]
        K = [ctx.enter_context(nc.psum_tensor(f"K{i}", [P, CH], F32)) for i in range(2)]
        L = ctx.enter_context(nc.psum_tensor("L", [P, CH], F32))
        Rb = ctx.enter_context(nc.psum_tensor("Rb", [P, CH], F32))
        U = K
        V = [L, Rb]
        TX, TH, HP, YP = K[0], K[1], L, Rb

        w13h = sb("w13h", [P, 2, KC, HS], F32R)
        w13l = sb("w13l", [P, 2, KC, HS], F32R)
        w2h = sb("w2h", [P, HC, D], F32R)
        w2l = sb("w2l", [P, HC, D], F32R)
        ident = sb("ident", [P, P])
        upper = sb("upper", [P, P])
        ones = sb("ones", [P, P])
        zeros = sb("zeros", [P, P])
        iota8 = sb("iota8", [P, E])
        iotap = sb("iotap", [P, 1])
        tb = sb("tb", [P, NB, E])
        rbias = sb("rbias", [P, E])
        rwhl = sb("rwhl", [P, KC, 2 * E], F32R)
        pos_all = sb("pos_all", [P, NT * TOPK])
        ypos = sb("ypos", [P, NT * TOPK], I32)
        gate_all = sb("gate_all", [P, NT * TOPK])
        pos_fix = sb("pos_fix", [P, 2, TT * TOPK], I32)
        gate_fix = sb("gate_fix", [P, TT * TOPK])
        tabi = sb("tabi", [P, 8], I32)
        tab = sb("tab", [P, 8])
        run = sb("run", [P, 2, TT + 1, E])
        sum16 = sb("sum16", [2 * E, E])

        over1 = ExitStack()
        x1h = sb("x1h", [P, KC, T], F32R, over1)
        x1l = sb("x1l", [P, KC, T], F32R, over1)
        over1.close()
        with ExitStack() as over1:
            xgh = sb("xgh", [P, KC, P], F32R, over1)
            xgl = sb("xgl", [P, KC, P], F32R, over1)
            hTh = sb("hTh", [P, KC, P], F32R, over1)
            hTl = sb("hTl", [P, KC, P], F32R, over1)
            hg = sb("hg", [P, HE], F32, over1)
            yo = sb("yo", [P, 2, D], F32, over1)
        over1 = ctx.enter_context(ExitStack())
        sb("over1_hold", [P, 2 * KC * T], F32, over1)

        with ExitStack() as st:
            basep = sb("basep", [P, KC, D], F32, st)
            xtok = sb("xtok", [P, TT, D], F32, st)
            wraw = sb("wraw", [P, PIECE], F32, st)
            with ExitStack() as z:
                w2c = sb("w2c", [P, RING, KC, CH], F32, z)
                b2c = sb("b2c", [8, RING, CH], F32, z)
                w1c = sb("w1c", [P, KC, D], F32, z)
                xwc = sb("xwc", [8, 2, RK, WPC], F32, z)
                craw = sb("craw", [8, D], F32, z)
                lng = sb("lng", [8, D], F32, z)
                lnb = sb("lnb", [8, D], F32, z)
                cb1b = sb("cb1b", [8, D], F32, z)
                ae = sb("ae", [8, D], F32, z)
                hc_ = sb("hcond", [8, D], F32, z)
                actT = sb("actT", [P, 3, KC, 8], F32, z)
                stats = sb("stats", [8, 16], F32, z)
                rwr = sb("rwr", [P, 2 * KC, E], F32, z)
                tbs = sb("tbs", [8, NB, E], F32, z)
            xTh = sb("xTh", [P, KC, T], F32R, st)
            xTl = sb("xTl", [P, KC, T], F32R, st)
            layf = sb("layf", [P, 2, D], F32, st)
            layh = sb("layh", [P, KC, D], F32R, st)
            layl = sb("layl", [P, KC, D], F32R, st)
            stkr = sb("stkr", [STACK, 2, D], F32, st)
            stk = sb("stk", [STACK, 2, D], F32R, st)
            x1T = sb("x1T", [P, KC, T], F32, st)
            x1tok = sb("x1tok", [P, 2, TT, D], F32, st)
            rs = [sb(f"rs{i}", [P, TT, TOPK, E], F32, st) for i in range(4)]
            zT = sb("zT", [2 * E, T], F32, st)
            mx = sb("mx", [P, TT, E], F32, st)
            mk = sb("mk", [P, TT + 1, E], F32, st)
            mi = sb("mi", [P, TT, E], U32, st)
            sg = sb("sg", [P, TT * TOPK], F32, st)
            msk = sb("msk", [P, TT, TOPK, E], F32, st)
        slf = sb("slf", [P, 2, T])
        gTh = sb("gTh", [P, 2, T], F32R)
        gTl = sb("gTl", [P, 2, T], F32R)
        tw = sb("tw", [P, 12, E])
        twi = sb("twi", [P, 4, E], I32)
        step = sb("step", [P, NT * TOPK])
        slots = sb("slots", [P, NT * TOPK])
        tab_i = sb("tab_i", [1, TAB * 8], I32)
        with ExitStack() as st:
            weraw = sb("weraw", [P, WSL], F32, st)
            xr = sb("xr", [P, 2, D], F32, st)
            weh = sb("weh", [P, 2, 2 * WSL], F32R, st)
            wel = sb("wel", [P, 2, 2 * WSL], F32R, st)
        with ExitStack() as st:
            x1raw = sb("x1raw", [P, KC * T], F32, st)
            xres = sb("xres", [P, TT, D], F32, st)
            yb = sb("yb", [P, TT * TOPK, D], F32, st)

        small_in = sem("small_in")
        w2c_in = [sem(f"w2c_in{i}") for i in range(RING)]
        wraw_in = sem("wraw_in")
        base_in = sem("base_in")
        consts = sem("consts")
        waited = {e.engine: sem(f"waited_{n}") for n, e in
                  (("sp", nc.sync), ("pool", nc.gpsimd), ("dve", nc.vector), ("act", nc.scalar), ("pe", nc.tensor))}
        d0 = sem("d0")
        p0 = sem("p0")
        a0 = sem("a0")
        xw_ps = sem("xw_ps")
        xw_sb = sem("xw_sb")
        xwc_out = [sem(f"xwc_out{i}") for i in range(2)]
        wsh = sem("wsh")
        wsl = sem("wsl")
        x_in = [sem(f"x_in{c}") for c in range(KC)]
        stk_in = sem("stk_in")
        stk_hi = sem("stk_hi")
        stk_lo = sem("stk_lo")
        xt_ps = sem("xt_ps")
        xt_hi = sem("xt_hi")
        xt_lo = sem("xt_lo")
        lay_ps = sem("lay_ps")
        lay_f = sem("lay_f")
        lay_hi = sem("lay_hi")
        lay_lo = sem("lay_lo")
        main_ps = sem("main_ps")
        x1_f = sem("x1_f")
        x1_hi = sem("x1_hi")
        x1_lo = sem("x1_lo")
        tok_ps = sem("tok_ps")
        tok_sb = sem("tok_sb")
        zt_ps = sem("zt_ps")
        zt_sb = sem("zt_sb")
        z_ps = sem("z_ps")
        z_sb = sem("z_sb")
        ez = sem("ez")
        masks = sem("masks")
        rank_ps = sem("rank_ps")
        pos_rdy = sem("pos_rdy")
        dr = sem("dr")
        x1T_out = sem("x1T_out")
        x1_out = [sem(f"x1_out{i}") for i in range(2)]
        scat = [sem(f"scat{i}") for i in range(2)]
        tabs = sem("tabs")
        dt_ = sem("dt")
        dy = sem("dy")
        pad_out = sem("pad_out")
        class Ffn:
            def __init__(self, tag):
                self.u_ps = sem(f"u_ps_{tag}")
                self.v_ps = sem(f"v_ps_{tag}")
                self.silu = sem(f"silu_{tag}")
                self.g_f = sem(f"g_f_{tag}")
                self.g_hi = sem(f"g_hi_{tag}")
                self.g_lo = sem(f"g_lo_{tag}")
                self.o_ps = sem(f"o_ps_{tag}")
                self.sum_ps = sem(f"sum_ps_{tag}")
        S, F = Ffn("s"), Ffn("f")
        places_all = sem("places_all")
        gates = sem("gates")
        tab_out = sem("tab_out")
        tab_in = sem("tab_in")
        xr_in = [sem(f"xr_in{i}") for i in range(2)]
        xg_ps = sem("xg_ps")
        xg_hi = sem("xg_hi")
        xg_lo = sem("xg_lo")
        h_ps = sem("h_ps")
        h_g = sem("h_g")
        ht_ps = sem("ht_ps")
        ht_hi = sem("ht_hi")
        ht_lo = sem("ht_lo")
        y_ps = sem("y_ps")
        y_sb = sem("y_sb")
        y_out = [sem(f"y_out{i}") for i in range(2)]
        weraw_in = sem("weraw_in")
        we_hi = sem("we_hi")
        we_lo = sem("we_lo")
        x1raw0_in = sem("x1raw0_in")
        x1raw_in = sem("x1raw_in")
        assert WSL == KC * T
        xres_in = sem("xres_in")
        xf_hi = sem("xf_hi")
        xf_lo = sem("xf_lo")
        pos_f = sem("pos_f")
        y_in = sem("y_in")
        gate_f = sem("gate_f")
        acc = sem("acc")
        comb = sem("comb")
        out_st = sem("out_st")

        block = ctx.enter_context(nc.Block())

        PIECE_AT = {(-1, 0): 0, (-1, 1): 1, (-1, 2): 2, (0, 1): 3, (0, 3): 4, (1, 2): 5, (1, 3): 6, (2, 2): 7, (2, 3): 8,
                    (NB - 1, 1): 9, (NB - 1, 2): 10, (NB - 1, 3): 11}
        assert len(PIECE_AT) == PIECES
        X_AFTER = {12: (0,), 13: (1,), 14: (2,), 15: (3,)}
        QUADS = 4
        TOK_BANK = (0, 1, 1, 0)
        RANKS = slice(64, 64 + (TT + 1) * E)
        D_VAR, D_AE, D_AET, D_HPRE, D_HT, D_TBS, D_TB = 3, 7, 9, 10, 11, 14, 15

        def value(eng, col, at, hi, lo=0):
            alone(eng)
            return eng.value_load(tab_i[0:1, ds(at * 8 + col, 1)], min_val=lo, max_val=hi)

        def blocks(eng, body, done):
            for b in range(3):
                body(b, b % 2)
            with eng.Fori(1, (NB - 2) // 2) as i:
                body(i * 2 + 1, 1)
                body(i * 2 + 2, 0)
            body(NB - 1, 1)
            done()

        def tiles(eng, pairs, body):
            body(0)
            with eng.Fori(1, pairs) as j:
                body(j)

        def alone(eng):
            eng.sem_inc(waited[eng.engine], 1)

        def first(b):
            return isinstance(b, int) and b == 0

        def last(b):
            return isinstance(b, int) and b == NB - 1

        def piece_of(w13, w2x, i):
            if i < 2 * KC:
                return w13[:, i // KC, i % KC]
            k = PIECE // D
            return w2x[:, (i - 2 * KC) * k:(i - 2 * KC + 1) * k].rearrange("p k n -> p (k n)")

        def piece_at(b, point, do):
            if isinstance(b, int) and (b, point) in PIECE_AT:
                do(PIECE_AT[b, point])

        def before(eng, ffn, b, h, none):
            if h >= 2:
                eng.wait_ge(ffn.o_ps, b * (HC - 1) + (h - 1))
            elif not none:
                eng.wait_ge(*((ffn.o_ps, b * (HC - 1)) if h == 0 else (ffn.sum_ps, b * TT)))

        def ffn_act(act, ffn, b, none):
            for h in range(HC):
                n = b * HC + h
                act.wait_ge(ffn.u_ps, n + 1)
                if h >= 2 or not none:
                    act.wait_ge(ffn.g_lo, n - 1)
                nc.scalar.activation(slf[:, h % 2], U[h % 2][:], ACT.Silu).then_inc(ffn.silu, 1)
                act.wait_ge(ffn.g_f, n + 1)
                before(act, ffn, b, h, none)
                nc.scalar.copy(gTh[:, h % 2], slf[:, h % 2]).then_inc(ffn.g_hi, 1)

        def ffn_dve(dve, ffn, b, after={}):
            for h in range(HC):
                n = b * HC + h
                dve.wait_ge(ffn.silu, n + 1)
                dve.wait_ge(ffn.v_ps, n + 1)
                nc.vector.tensor_tensor(slf[:, h % 2], V[h % 2][:], slf[:, h % 2], ALU.mult).then_inc(ffn.g_f, 1)
                dve.wait_ge(ffn.g_hi, n + 1)
                nc.vector.tensor_tensor(gTl[:, h % 2], slf[:, h % 2], gTh[:, h % 2].bitcast(F32),
                                        ALU.subtract).then_inc(ffn.g_lo, 1)
                if h in after:
                    after[h]()

        def store_factors(sp, n):
            ab, w0 = n // (NCH // 2), n % (NCH // 2) * WPC
            sp.dma_start(xw_d[:, ab, :, w0:w0 + WPC], xwc[:, n % 2]).then_inc(xwc_out[n % 2], 16)

        def load_piece(sp, i):
            if i > 0:
                sp.wait_ge(wsh, i)
                sp.wait_ge(wsl, i)
            if i < 2 * KC:
                src = (w1, w3)[i // KC][i % KC * P:(i % KC + 1) * P, :]
                sp.dma_start(wraw[:], src).then_inc(wraw_in, 16)
            else:
                k = PIECE // D
                src = w2.rearrange("(k p) n -> p k n", p=P)[:, (i - 2 * KC) * k:(i - 2 * KC + 1) * k, :]
                sp.dma_start(wraw[:].rearrange("p (k n) -> p k n", k=k), src).then_inc(wraw_in, 16)

        def load_stack(sp, b):
            for g in GROUPS:
                sp.dma_start(stkr[g:g + RK], xw_d[ds(b, 1)].rearrange("b a r d -> (b r) a d")
                             ).then_inc(stk_in, 16)

        @block.sync
        def _(sp):
            for dst, src in ((craw[:], cond), (lng[:], row_bc(ln_g, 8)), (lnb[:], row_bc(ln_b, 8)),
                             (w1c[:], cw1.rearrange("(k p) n -> p k n", p=P)),
                             (cb1b[:], row_bc(cb1, 8)),
                             (rwr[:], rw.rearrange("(k p) e -> p k e", p=P)),
                             (rbias[:], row_bc(rb, P))):
                sp.dma_start(dst, src).then_inc(small_in, 16)
            for n in range(NCH):
                r = n % RING
                if n >= RING:
                    sp.wait_ge(xw_sb, n - RING + 1)
                    store_factors(sp, n - RING)
                sp.dma_start(w2c[:, r], cw2_view[:, :, n * CH:(n + 1) * CH]).then_inc(w2c_in[r], 16)
                sp.dma_start(b2c[:, r], row_bc(cb2[n * CH:(n + 1) * CH], 8)).then_inc(w2c_in[r], 16)
                if n == RING - 1:
                    load_piece(sp, 0)
                    load_piece(sp, 1)
                for c in X_AFTER.get(n, ()):
                    sp.dma_start(xtok[:, :, c * P:(c + 1) * P],
                                 x_view[:, 0:TT, c * P:(c + 1) * P]).then_inc(x_in[c], 16)
            for n in range(NCH - RING, NCH):
                if n == NCH - 2:
                    sp.dma_start(basep[:], base.rearrange("(k p) n -> p k n", p=P)).then_inc(base_in, 16)
                sp.wait_ge(xw_sb, n + 1)
                store_factors(sp, n)
            for i in range(2):
                sp.wait_ge(xwc_out[i], 16 * NCH // 2)
            sp.wait_ge(consts, 8)
            load_stack(sp, 0)
            load_piece(sp, 2)

            def store_tok(b, slot):
                sp.wait_ge(tok_sb, b * TT + TT)
                sp.dma_start(x1_view[:, ds(b * TT, TT), :], x1tok[:, slot]).then_inc(x1_out[slot], 16)

            def body(b, slot):
                if not last(b):
                    sp.wait_ge(stk_hi, b + 1)
                    sp.wait_ge(stk_lo, b * 2 + 2)
                    load_stack(sp, b + 1)
                piece_at(b, 1, lambda i: load_piece(sp, i))
                if not last(b):
                    piece_at(b, 2, lambda i: load_piece(sp, i))
                for c in range(KC):
                    if c == 3 and not first(b):
                        store_tok(b - 1, 1 - slot)
                    if not last(b):
                        sp.wait_ge(xt_ps, b * KC + c + 1)
                        sp.dma_start(xtok[:, :, c * P:(c + 1) * P],
                                     x_view[:, ds((b + 1) * TT, TT), c * P:(c + 1) * P]).then_inc(x_in[c], 16)
                if last(b):
                    piece_at(b, 2, lambda i: load_piece(sp, i))
                piece_at(b, 3, lambda i: load_piece(sp, i))
                sp.wait_ge(x1_f, b * KC + KC)
                sp.dma_start(x1T_d[:, ds(b, 1), :].rearrange("p b n -> p (b n)"),
                             x1T[:].rearrange("p k n -> p (k n)")).then_inc(x1T_out, 16)

            def done():
                store_tok(NB - 1, 1)
                zero_src = zeros[:].unsqueeze(1).broadcast_to([P, KC, P])

                def zero_rows(row):
                    return xs_d[ds(row, P), :].rearrange("r (k c) -> r k c", k=KC)
                sp.wait_ge(consts, 8)
                sp.dma_start(zero_rows(E * REGION), zero_src).then_inc(pad_out, 16)
                for t in range(N * TOPK // P, 2 * PAIRS_MAX):
                    sp.dma_start(ys_d[t * P:(t + 1) * P, :].rearrange("r (k c) -> r k c", k=KC), zero_src).then_inc(pad_out, 16)
                sp.wait_ge(tabs, 1)
                sp.dma_start(tab_d, tabi[0:TAB]).then_inc(tab_out, 16)
                sp.wait_ge(tab_out, 16)
                sp.dma_start(tab_i[:], tab_d.rearrange("(a p) c -> a (p c)", a=1)).then_inc(tab_in, 16)
                sp.wait_ge(tab_in, 16)
                with sp.Fori(0, E) as e:
                    row = value(sp, PAD, e, E * REGION - P)
                    sp.dma_start(zero_rows(row), zero_src).then_inc(pad_out, 16)
                sp.wait_ge(pad_out, 16 * (E + 1 + 2 * PAIRS_MAX - N * TOPK // P))
                for s in range(2):
                    sp.wait_ge(scat[s], 16 * TT * TOPK * NB // 2)

            blocks(sp, body, done)
            for s in range(2):
                sp.wait_ge(x1_out[s], 16 * NB // 2)
            sp.wait_ge(x1T_out, 16 * NB)
            def load_rows(t, slot):
                row = value(sp, ROW, t, E * REGION)
                sp.dma_start(xr[:, slot], xs_d[ds(row, P), :]).then_inc(xr_in[slot], 16)
            load_rows(0, 0)
            load_rows(1, 1)
            sp.wait_ge(xg_ps, 1)
            load_rows(2, 0)
            sp.wait_ge(xg_ps, 2)
            load_rows(3, 1)
            pairs = value(sp, PAIRS, 0, PAIRS_MAX, 1)

            def rpair(j):
                for s in range(2):
                    t = j * 2 + s
                    sp.wait_ge(xg_ps, t + 3)
                    load_rows(t + 4, s)
                    sp.wait_ge(y_sb, t + 1)
                    alone(sp)
                    sp.dma_start(ys_d[ds(t * P, P), :], yo[:, s]).then_inc(y_out[s], 16)
            tiles(sp, pairs, rpair)
            for s in range(2):
                sp.wait_ge(xr_in[s], pairs * 16 + 32)
                alone(sp)
            sp.wait_ge(y_ps, pairs * 2 + 1)
            alone(sp)
            sp.dma_start(xres[:], x1_view[:, (NB - 1) * TT:NB * TT, :]).then_inc(xres_in, 16)
            sp.wait_ge(comb, TT)
            sp.dma_start(out_view[:, (NB - 1) * TT:NB * TT, :], xres[:]).then_inc(out_st, 16)

            def fblock(b, ends):
                sp.wait_ge(out_st, (b + 1) * 16)
                alone(sp)
                sp.dma_start(xres[:], x1_view[:, ds(b * TT, TT), :]).then_inc(xres_in, 16)
                if not ends:
                    sp.wait_ge(xf_hi, b * KC + KC)
                    sp.wait_ge(xf_lo, b * KC + KC)
                    alone(sp)
                    sp.dma_start(x1raw[:], x1T_d[:, ds(b + 1, 1), :].rearrange("p b n -> p (b n)")
                                 ).then_inc(x1raw_in, 16)
                if not ends:
                    sp.wait_ge(comb, b * TT + 2 * TT)
                    alone(sp)
                    sp.dma_start(out_view[:, ds(b * TT, TT), :], xres[:]).then_inc(out_st, 16)
                for t in range(TT if ends else 0):
                    sp.wait_ge(comb, (b + 1) * TT + t + 1)
                    sp.dma_start(out_view[:, b * TT + t:b * TT + t + 1, :], xres[:, t:t + 1]).then_inc(out_st, 16)
            with sp.Fori(0, NB - 2) as b:
                fblock(b, False)
            fblock(NB - 2, True)
            sp.wait_ge(out_st, 16 * (NB - 1 + TT))

        @block.gpsimd
        def _(pool):
            nc.gpsimd.memset(ident[:], 0.0).then_inc(consts, 1)
            nc.gpsimd.memset(ones[:], 1.0).then_inc(consts, 1)
            pool.wait_ge(consts, 2)
            nc.gpsimd.affine_select(out=ident[:], in_=ident[:], compare_op=ALU.not_equal, fill=1.0, base=0,
                                    pattern=[[-1, P]], channel_multiplier=1).then_inc(consts, 1)
            nc.gpsimd.affine_select(out=upper[:], in_=ones[:], compare_op=ALU.is_gt, fill=0.0, base=0,
                                    pattern=[[1, P]], channel_multiplier=-1).then_inc(consts, 1)
            nc.gpsimd.iota(iota8[:], pattern=[[1, E]], base=0, channel_multiplier=0,
                           allow_small_or_imprecise_dtypes=True).then_inc(consts, 1)
            nc.gpsimd.iota(iotap[:], pattern=[[1, 1]], base=0, channel_multiplier=1,
                           allow_small_or_imprecise_dtypes=True).then_inc(consts, 1)
            nc.gpsimd.memset(zeros[:], 0.0).then_inc(consts, 1)
            pool.wait_ge(xw_ps, NCH)
            pool.wait_ge(xw_sb, NCH)
            pool.wait_ge(p0, 5)
            nc.gpsimd.memset(stkr[:], 0.0).then_inc(consts, 1)

            def scatter(b, slot):
                pool.wait_ge(pos_rdy, b + 1)
                pool.wait_ge(tok_sb, b * TT + TT)
                alone(pool)
                for t in range(TT):
                    for k in range(TOPK):
                        c = t * TOPK + k
                        pool.indirect_dma_start(
                            out=xs_d, out_offset=bass.IndirectOffsetOnAxis(ap=pos_fix[:, slot, c:c + 1].bitcast(U32), axis=0),
                            in_=x1tok[:, slot, t, :], in_offset=None).then_inc(scat[slot], 16)

            def body(b, slot):
                for c in range(0, KC, 2 if last(b) else 1):
                    pool.wait_ge(x1_hi, b * KC + c + 1)
                    nc.gpsimd.tensor_tensor(x1l[:, c], x1T[:, c], x1h[:, c].bitcast(F32),
                                            ALU.subtract).then_inc(x1_lo, 1)
                if not first(b):
                    scatter(b - 1, 1 - slot)

            def done():
                scatter(NB - 1, (NB - 1) % 2)

            blocks(pool, body, done)
            pool.wait_ge(tab_in, 16)
            for s in range(2):
                pool.wait_ge(scat[s], 16 * TT * TOPK * NB // 2)
                pool.wait_ge(x1_out[s], 16 * NB // 2)
            pool.wait_ge(x1T_out, 16 * NB)
            nact = value(pool, NACT, 0, E, 2)

            def cut_expert(k):
                arow = value(pool, AROW, k, (E - 1) * KC)
                free = value(pool, FREE, k, P)
                off = (k & 1) * WSL
                pool.wait_ge(y_ps, free + 1)
                for m, view in ((0, w1e_view), (1, w2e_view)):
                    raw = weraw[:].rearrange("p (k n) -> p k n", k=KC)
                    if not (first(k) and m == 0):
                        pool.wait_ge(we_lo, k * 2 + m)
                    alone(pool)
                    pool.dma_start(raw, view[:, ds(arow, KC), :]).then_inc(weraw_in, 16)
                    pool.wait_ge(weraw_in, k * 32 + 16 * m + 16)
                    alone(pool)
                    hi, lo = weh[:, m, ds(off, WSL)], wel[:, m, ds(off, WSL)]
                    nc.gpsimd.tensor_copy(hi, weraw[:]).then_inc(we_hi, 1)
                    pool.wait_ge(we_hi, k * 2 + m + 1)
                    nc.gpsimd.tensor_tensor(lo, weraw[:], hi.bitcast(F32), ALU.subtract).then_inc(we_lo, 1)
            cut_expert(0)
            with pool.Fori(1, nact) as k:
                cut_expert(k)
            pool.wait_ge(we_lo, nact * 2)
            alone(pool)
            pool.dma_start(x1raw[:], x1T_d[:, 0:1, :].rearrange("p b n -> p (b n)")).then_inc(x1raw0_in, 16)
            pairs = value(pool, PAIRS, 0, PAIRS_MAX, 1)
            pool.wait_ge(tabs, 3)
            for s in range(2):
                pool.wait_ge(y_out[s], pairs * 16)
            pool.wait_ge(y_ps, pairs * 2 + 1)
            alone(pool)

            def gather(b, m):
                nc.gpsimd.tensor_copy(pos_fix[:, 0], ypos[:, ds(b * (TT * TOPK), TT * TOPK)]).then_inc(pos_f, 1)
                pool.wait_ge(pos_f, m + 1)
                if not (isinstance(m, int) and m == 0):
                    pool.wait_ge(comb, m * TT)
                alone(pool)
                for c in range(TT * TOPK):
                    pool.indirect_dma_start(
                        out=yb[:, c, :], out_offset=None, in_=ys_d,
                        in_offset=bass.IndirectOffsetOnAxis(ap=pos_fix[:, 0, c:c + 1].bitcast(U32), axis=0)
                    ).then_inc(y_in, 16)
                pool.wait_ge(y_in, (m + 1) * (16 * TT * TOPK))

            gather(NB - 1, 0)
            with pool.Fori(0, NB - 1) as b:
                gather(b, b + 1)

        @block.scalar
        def _(act):
            def cut_piece(i):
                act.wait_ge(wraw_in, 16 * (i + 1))
                nc.scalar.copy(piece_of(w13h, w2h, i), wraw[:]).then_inc(wsh, 1)

            act.wait_ge(d0, D_VAR)
            nc.scalar.activation(stats[:, 9:10], stats[:, 8:9], ACT.Sqrt).then_inc(a0, 1)
            act.wait_ge(d0, D_HPRE)
            nc.scalar.activation(hc_[:], ae[:], ACT.Gelu).then_inc(a0, 1)
            act.wait_ge(small_in, 16 * 7)
            nc.scalar.copy(rwhl[:, :, 0:E], rwr[:, 0:KC, :]).then_inc(a0, 1)
            for i in range(2):
                piece_at(-1, i, cut_piece)

            def cut_stack(b):
                act.wait_ge(stk_in, b * 48 + 48)
                if not first(b):
                    act.wait_ge(lay_ps, b * KC)
                nc.scalar.copy(stk[:], stkr[:]).then_inc(stk_hi, 1)

            def cut_xt(b, c):
                act.wait_ge(xt_ps, b * KC + c + 1)
                nc.scalar.copy(xTh[:, c], K[c % 2][:]).then_inc(xt_hi, 1)

            def cut_layer(b, c):
                act.wait_ge(lay_f, b * KC + c + 1)
                nc.scalar.copy(layh[:, c], layf[:, c % 2]).then_inc(lay_hi, 1)

            def exp_scores(b):
                act.wait_ge(z_sb, b + 1)
                nc.scalar.activation(rs[1][:, :, 0], rs[0][:, :, 0], ACT.Exp, scale=-1.0).then_inc(ez, 1)

            def keep_tok(b, slot, t):
                act.wait_ge(tok_ps, b * TT + t + 1)
                nc.scalar.copy(x1tok[:, slot, t], K[TOK_BANK[t]][:]).then_inc(tok_sb, 1)

            def keep_scores(b):
                act.wait_ge(zt_ps, b + 1)
                nc.scalar.copy(zT[:], Rb[0:2 * E, :]).then_inc(zt_sb, 1)

            act.wait_ge(xw_ps, NCH)
            cut_stack(0)
            act.wait_ge(xw_sb, NCH)
            for c in range(2):
                cut_xt(0, c)
                cut_layer(0, c)
            piece_at(-1, 2, cut_piece)

            def body(b, slot):
                cut_xt(b, 2)
                cut_layer(b, 2)
                piece_at(b, 1, cut_piece)
                if not first(b):
                    keep_tok(b - 1, 1 - slot, 2)
                    keep_tok(b - 1, 1 - slot, 3)
                cut_xt(b, 3)
                if not first(b):
                    keep_scores(b - 1)
                cut_layer(b, 3)
                piece_at(b, 2, cut_piece)
                if not last(b):
                    cut_stack(b + 1)
                if not first(b):
                    exp_scores(b - 1)
                    act.wait_ge(x1T_out, b * 16)
                    act.wait_ge(x1_lo, b * KC)
                if not last(b):
                    cut_xt(b + 1, 0)
                for c in range(KC):
                    act.wait_ge(main_ps, b * KC + c + 1)
                    nc.scalar.copy(x1T[:, c], M[c][:]).then_inc(x1_f, 1)
                if not last(b):
                    cut_xt(b + 1, 1)
                    cut_layer(b + 1, 0)
                    cut_layer(b + 1, 1)
                wait_slot(b, slot)
                for c in range(KC):
                    if c >= 2:
                        keep_tok(b, slot, c - 2)
                    if c == 0:
                        act.wait_ge(x1_f, b * KC + KC)
                    nc.scalar.copy(x1h[:, c], x1T[:, c]).then_inc(x1_hi, 1)
                piece_at(b, 3, cut_piece)

            def wait_slot(b, slot):
                half = (b - slot) >> 1
                if isinstance(b, int) and half == 0:
                    return
                act.wait_ge(scat[slot], half * (16 * TT * TOPK))
                act.wait_ge(x1_out[slot], half * 16)

            def done():
                keep_tok(NB - 1, 1, 2)
                keep_tok(NB - 1, 1, 3)
                keep_scores(NB - 1)
                exp_scores(NB - 1)

            blocks(act, body, done)
            ffn_act(act, S, 0, True)
            def cut_x(n):
                act.wait_ge(xg_ps, n)
                nc.scalar.copy(xgh[:].rearrange("p k n -> p (k n)"), TX[:]).then_inc(xg_hi, 1)

            def gelu(n):
                act.wait_ge(h_ps, n)
                nc.scalar.activation(hg[:], HP[:], ACT.Gelu).then_inc(h_g, 1)

            def cut_h(n):
                act.wait_ge(ht_ps, n)
                nc.scalar.copy(hTh[:].rearrange("p k n -> p (k n)"), TH[:]).then_inc(ht_hi, 1)

            act.wait_ge(S.g_lo, HC)
            act.wait_ge(tab_in, 16)
            cut_x(1)
            gelu(1)
            cut_x(2)
            cut_h(1)
            pairs = value(act, PAIRS, 0, PAIRS_MAX, 1)

            def rpair(j):
                for s in range(2):
                    t = j * 2 + s
                    gelu(t + 2)
                    cut_x(t + 3)
                    cut_h(t + 2)
            tiles(act, pairs, rpair)
            act.wait_ge(ht_lo, pairs * 2 + 1)
            act.wait_ge(xg_lo, pairs * 2 + 2)
            act.wait_ge(y_ps, pairs * 2 + 1)

            def fblock(b):
                if first(b):
                    act.wait_ge(x1raw0_in, 16)
                else:
                    act.wait_ge(x1raw_in, b * 16)
                    act.wait_ge(F.v_ps, b * HC)
                for c in range(KC):
                    nc.scalar.copy(x1h[:, c], x1raw[:, c * T:(c + 1) * T]).then_inc(xf_hi, 1)
                ffn_act(act, F, b, first(b))
            fblock(0)
            with act.Fori(1, NB - 1) as b:
                fblock(b)

        def tables(dve):
            n = [0]

            def link(ins):
                n[0] += 1
                ins.then_inc(dt_, 1)
                dve.wait_ge(dt_, n[0])

            tt, ts, red = nc.vector.tensor_tensor, nc.vector.tensor_scalar, nc.vector.tensor_reduce
            cnt, nt, active, ends, ranks, past, rows, t7, t8, t9 = (tw[:, i] for i in range(10))
            col = [tab[:, i:i + 1] for i in range(8)]
            tmp = [tw[:, 10, i:i + 1] for i in range(4)]
            ti = [twi[:, 1, i:i + 1] for i in range(4)]
            link(nc.vector.scalar_tensor_tensor(out=cnt, in0=iota8[:], scalar=-float(REGION), in1=run[:, 1, TT],
                                                op0=ALU.mult, op1=ALU.add))
            link(ts(twi[:, 0], cnt, float(P - 1), None, ALU.add))
            link(ts(twi[:, 0], twi[:, 0], 7, None, ALU.logical_shift_right))
            link(nc.vector.tensor_copy(nt, twi[:, 0]))
            link(ts(active, nt, 0.0, None, ALU.is_gt))
            link(nc.vector.tensor_tensor_scan(ends, ones[:, 0:E], nt, 0.0, ALU.mult, ALU.add))
            link(nc.vector.tensor_tensor_scan(ranks, ones[:, 0:E], active, 0.0, ALU.mult, ALU.add))
            link(ts(past, ends, iotap[:, 0:1], None, ALU.is_le))
            link(ts(rows, nt, -float(P), float(REGION), ALU.mult, ALU.add))
            link(tt(rows, rows, past, ALU.mult))
            link(red(tmp[0], rows, AX, ALU.add))
            link(nc.vector.scalar_tensor_tensor(out=tmp[0], in0=iotap[:], scalar=float(P), in1=tmp[0],
                                                op0=ALU.mult, op1=ALU.add))
            link(ts(col[ROW], tmp[0], float(E * REGION), None, ALU.min))
            link(tt(t7, active, past, ALU.mult))
            link(red(tmp[1], t7, AX, ALU.add))
            link(nc.vector.tensor_copy(col[NACT], ranks[:, E - 1:E]))
            link(ts(tmp[2], col[NACT], -1.0, None, ALU.add))
            link(tt(tmp[1], tmp[1], tmp[2], ALU.min))
            link(ts(col[WCNT], tmp[1], 2.0, 1.0, ALU.mult, ALU.add))
            link(nc.vector.tensor_copy(ti[0], tmp[1]))
            link(ts(ti[0], ti[0], 1, None, ALU.bitwise_and))
            link(nc.vector.tensor_copy(tmp[1], ti[0]))
            link(ts(col[WOFF], tmp[1], float(WSL), None, ALU.mult))
            link(ts(t7, ranks, iotap[:, 0:1], None, ALU.is_le))
            link(red(tmp[3], t7, AX, ALU.add))
            link(ts(col[AROW], tmp[3], float(E - 1), float(KC), ALU.min, ALU.mult))
            link(ts(t8, ranks, iotap[:, 0:1], None, ALU.is_lt))
            link(tt(t8, t8, nt, ALU.mult))
            link(red(col[FREE], t8, AX, ALU.add))
            link(tt(t9, ident[:, 0:E], run[:, 1, TT], ALU.mult))
            link(red(col[PAD], t9, AX, ALU.add))
            link(ts(ti[1], ends[:, E - 1:E], 1.0, None, ALU.add))
            link(ts(ti[1], ti[1], 1, None, ALU.logical_shift_right))
            link(nc.vector.tensor_copy(col[PAIRS], ti[1]))
            nc.vector.tensor_copy(tabi[:], tab[:]).then_inc(tabs, 1)
            nc.vector.tensor_scalar(t9, nt, float(P), -float(REGION), ALU.mult, ALU.add).then_inc(tabs, 1)

        def rows_in_ys(dve):
            n = [0]

            def link(ins):
                n[0] += 1
                ins.then_inc(dy, 1)
                dve.wait_ge(dy, n[0])

            tt, ts = nc.vector.tensor_tensor, nc.vector.tensor_scalar
            t9 = tw[:, 9]
            dve.wait_ge(tabs, 2)
            link(nc.vector.tensor_copy(slots[:], pos_all[:]))
            for e in range(1, E):
                link(ts(step[:], pos_all[:], float(e * REGION), t9[:, e - 1:e], ALU.is_ge, ALU.mult))
                link(tt(slots[:], slots[:], step[:], ALU.add))
            nc.vector.tensor_copy(ypos[:], slots[:]).then_inc(tabs, 1)

        def gate_weights(dve):
            n = [0]

            def link(ins):
                n[0] += 1
                ins.then_inc(gates, 1)
                dve.wait_ge(gates, n[0])

            tt, ts = nc.vector.tensor_tensor, nc.vector.tensor_scalar
            gall = gate_all[:].rearrange("p (t k) -> p t k", k=TOPK)
            den, r = step[:, 0:NT], step[:, NT:2 * NT]
            c, h = slots[:, 0:NT], slots[:, NT:2 * NT]
            dve.wait_ge(tabs, 3)
            link(tt(den, gall[:, :, 0], gall[:, :, 1], ALU.add))
            link(ts(r, den, GATE_EPS, None, ALU.add))
            link(ts(c, den, GATE_EPS, None, ALU.is_gt))
            link(nc.vector.reciprocal(r, r))
            link(ts(h, c, -0.5 / 3, 0.5 / 3, ALU.mult, ALU.add))
            link(nc.vector.scalar_tensor_tensor(out=r, in0=r, scalar=1.0 / 3, in1=c, op0=ALU.mult, op1=ALU.mult))
            link(tt(gall, gall, r.unsqueeze(2).broadcast_to([P, NT, TOPK]), ALU.mult))
            link(tt(gall, gall, h.unsqueeze(2).broadcast_to([P, NT, TOPK]), ALU.add))

        @block.vector
        def _(dve):
            tt, ts = nc.vector.tensor_tensor, nc.vector.tensor_scalar
            n0 = [0]

            def link(ins):
                n0[0] += 1
                ins.then_inc(d0, 1)
                dve.wait_ge(d0, n0[0])

            def cut_piece(i):
                dve.wait_ge(wsh, i + 1)
                tt(piece_of(w13l, w2l, i), wraw[:], piece_of(w13h, w2h, i).bitcast(F32),
                   ALU.subtract).then_inc(wsl, 1)

            dve.wait_ge(small_in, 16 * 7)
            link(nc.vector.bn_stats(stats[:, 0:6], craw[:]))
            link(nc.vector.bn_aggr(stats[:, 6:8], stats[:, 0:6]))
            link(ts(stats[:, 8:9], stats[:, 7:8], LN_EPS, None, ALU.add))
            assert n0[0] == D_VAR
            dve.wait_ge(a0, 1)
            link(nc.vector.reciprocal(stats[:, 10:11], stats[:, 9:10]))
            link(ts(ae[:], craw[:], stats[:, 6:7], stats[:, 10:11], ALU.subtract, ALU.mult))
            link(tt(ae[:], ae[:], lng[:], ALU.mult))
            link(tt(ae[:], ae[:], lnb[:], ALU.add))
            assert n0[0] == D_AE
            dve.wait_ge(p0, 1)
            link(nc.vector.tensor_copy(actT[:, 0].rearrange("p k b -> p (k b)"), K[0][:, 0:KC * 8]))
            dve.wait_ge(p0, 2)
            link(nc.vector.tensor_copy(actT[:, 1].rearrange("p k b -> p (k b)"), K[1][:, 0:KC * 8]))
            dve.wait_ge(p0, 3)
            link(tt(ae[:], L[0:8, :], cb1b[:], ALU.add))
            assert n0[0] == D_HPRE
            dve.wait_ge(p0, 4)
            link(nc.vector.tensor_copy(actT[:, 2].rearrange("p k b -> p (k b)"), K[0][:, 0:KC * 8]))
            assert n0[0] == D_HT
            dve.wait_ge(a0, 3)
            link(tt(rwhl[:, :, E:2 * E], rwr[:, 0:KC, :], rwhl[:, :, 0:E].bitcast(F32), ALU.subtract))
            dve.wait_ge(p0, 5)
            link(nc.vector.tensor_copy(stats[:, 8:16], Rb[0:8, 0:E]))
            dve.wait_ge(consts, 7)
            link(tt(tbs[:], ident[0:8, 0:NB].unsqueeze(2).broadcast_to([8, NB, E]),
                    stats[:, 8:16].unsqueeze(1).broadcast_to([8, NB, E]), ALU.mult))
            assert n0[0] == D_TBS
            dve.wait_ge(p0, 6)
            link(nc.vector.tensor_copy(tb[:].rearrange("p b e -> p (b e)"), Rb[:, 64:64 + NB * E]))
            assert n0[0] == D_TB
            piece_at(-1, 0, cut_piece)
            for n in range(NCH):
                dve.wait_ge(xw_ps, n + 1)
                if n >= 2:
                    dve.wait_ge(xwc_out[n % 2], 16 * (n // 2))
                for q in range(QUADS):
                    ws = slice(q * WPC // QUADS, (q + 1) * WPC // QUADS)
                    ins = tt(xwc[:, n % 2, :, ws].rearrange("b r w -> b w r"),
                             M[n % 2][32 * q:32 * q + 8, 0:P].rearrange("b (w r) -> b w r", r=RK),
                             b2c[:, n % RING, q * P:(q + 1) * P].rearrange("b (w r) -> b w r", r=RK), ALU.add)
                ins.then_inc(xw_sb, 1)
                if n == 1:
                    piece_at(-1, 1, cut_piece)
            dve.wait_ge(base_in, 16)
            for c in range(KC):
                v = basep[:, c, c * P:(c + 1) * P]
                nc.vector.scalar_tensor_tensor(out=v, in0=ident[:], scalar=2.0, in1=v,
                                               op0=ALU.mult, op1=ALU.add).then_inc(dr, 1)
            ts(run[:, 1, TT], iota8[:], float(REGION), None, ALU.mult).then_inc(dr, 1)
            tt(sum16[:], ident[0:2 * E, 0:E], ident[0:2 * E, E:2 * E], ALU.add).then_inc(dr, 1)
            ts(mk[:, TT], iota8[:], 0.0, None, ALU.mult).then_inc(dr, 1)
            DR0 = 7
            dve.wait_ge(dr, DR0)

            def cut_xt(b, c):
                dve.wait_ge(xt_hi, b * KC + c + 1)
                tt(xTl[:, c], K[c % 2][:], xTh[:, c].bitcast(F32), ALU.subtract).then_inc(xt_lo, 1)

            def add_base(b, c):
                dve.wait_ge(lay_ps, b * KC + c + 1)
                tt(layf[:, c % 2], L[:], basep[:, c], ALU.add).then_inc(lay_f, 1)

            def cut_layer(b, c):
                dve.wait_ge(lay_hi, b * KC + c + 1)
                tt(layl[:, c], layf[:, c % 2], layh[:, c].bitcast(F32), ALU.subtract).then_inc(lay_lo, 1)

            CHOICE, WEIGHTS, PLACES = 5 + 2 * TT, 2, 2
            CHAIN = CHOICE + WEIGHTS + PLACES
            z, e_, s = (rs[i][:, :, 0] for i in range(3))

            def chain(b, start):
                k = [start]

                def step(ins):
                    k[0] += 1
                    ins.then_inc(dr, 1)

                def link(ins):
                    step(ins)
                    dve.wait_ge(dr, b * CHAIN + (DR0 + k[0]))
                return k, step, link

            def add_condition(b):
                dve.wait_ge(z_ps, b + 1)
                tt(z, Rb[:, 0:TT * E].rearrange("p (t e) -> p t e", t=TT),
                   tb[:, ds(b, 1), :].broadcast_to([P, TT, E]), ALU.add).then_inc(z_sb, 1)

            def choose(b):
                k, step, link = chain(b, 0)
                dve.wait_ge(ez, b + 1)
                link(ts(e_, e_, 1.0, None, ALU.add))
                link(nc.vector.reciprocal(s, e_))
                link(tt(z, s, rbias[:].unsqueeze(1).broadcast_to([P, TT, E]), ALU.add))
                alone(dve)
                for t in range(TT):
                    (step if t < TT - 1 else link)(nc.vector.max(mx[:, t], z[:, t]))
                alone(dve)
                for t in range(TT):
                    (step if t < TT - 1 else link)(nc.vector.max_index(mi[:, t], mx[:, t], z[:, t]))
                link(nc.vector.tensor_copy(mx[:], mi[:]))
                link(tt(msk[:], iota8[:].unsqueeze(1).unsqueeze(1).broadcast_to([P, TT, TOPK, E]),
                        mx[:, :, 0:TOPK].unsqueeze(3).broadcast_to([P, TT, TOPK, E]), ALU.is_equal))
                tt(mk[:, 0:TT], msk[:, :, 0], msk[:, :, 1], ALU.add).then_inc(masks, 1)
                assert k[0] == CHOICE, k[0]

            def weigh(b):
                k, step, link = chain(b, CHOICE)
                link(tt(rs[3][:], msk[:], s.unsqueeze(2).broadcast_to([P, TT, TOPK, E]), ALU.mult))
                link(nc.vector.tensor_reduce(
                    gate_all[:, ds(b * (TT * TOPK), TT * TOPK)].rearrange("p (t k) -> p t k", k=TOPK),
                    rs[3][:], AX, ALU.add))
                assert k[0] == CHOICE + WEIGHTS, k[0]

            def places(b, slot):
                k, step, link = chain(b, CHOICE + WEIGHTS)
                dve.wait_ge(rank_ps, b + 1)
                link(tt(run[:, slot], Rb[:, RANKS].rearrange("p (t e) -> p t e", e=E),
                        run[:, 1 - slot, TT].unsqueeze(1).broadcast_to([P, TT + 1, E]), ALU.add))
                link(tt(rs[3][:], msk[:], run[:, slot, 0:TT].unsqueeze(2).broadcast_to([P, TT, TOPK, E]), ALU.mult))
                pf = sg[:].rearrange("p (t k) -> p t k", k=TOPK)
                nc.vector.tensor_reduce(pf, rs[3][:], AX, ALU.add).then_inc(masks, 1)
                assert k[0] == CHAIN, k[0]

            def store_places(b, slot):
                dve.wait_ge(masks, b * 2 + 2)
                nc.vector.tensor_copy(pos_all[:, ds(b * (TT * TOPK), TT * TOPK)], sg[:]).then_inc(places_all, 1)
                half = (b - slot) >> 1
                if not isinstance(b, int) or half > 0:
                    dve.wait_ge(scat[slot], half * (16 * TT * TOPK))
                nc.vector.tensor_copy(pos_fix[:, slot], sg[:]).then_inc(pos_rdy, 1)

            def cut_stack(b):
                dve.wait_ge(stk_hi, b + 1)
                for a, g in ((0, GROUPS[1]), (1, GROUPS[2])):
                    s = stk[g:g + RK, a]
                    tt(s, stkr[g:g + RK, a], s.bitcast(F32), ALU.subtract).then_inc(stk_lo, 1)

            cut_stack(0)
            for c in range(2):
                cut_xt(0, c)
                add_base(0, c)
                cut_layer(0, c)
            piece_at(-1, 2, cut_piece)

            def body(b, slot):
                for c in (2, 3):
                    if c == 3:
                        piece_at(b, 1, cut_piece)
                    cut_xt(b, c)
                    add_base(b, c)
                    cut_layer(b, c)
                if not first(b):
                    add_condition(b - 1)
                piece_at(b, 2, cut_piece)
                if not last(b):
                    cut_stack(b + 1)
                if not first(b):
                    choose(b - 1)
                if not last(b):
                    cut_xt(b + 1, 0)
                    add_base(b + 1, 0)
                    cut_xt(b + 1, 1)
                    cut_layer(b + 1, 0)
                    add_base(b + 1, 1)
                    cut_layer(b + 1, 1)
                if not first(b):
                    weigh(b - 1)
                    places(b - 1, 1 - slot)
                    store_places(b - 1, 1 - slot)
                if not last(b):
                    piece_at(b, 3, cut_piece)
                else:
                    for c in range(1, KC, 2):
                        dve.wait_ge(x1_hi, b * KC + c + 1)
                        tt(x1l[:, c], x1T[:, c], x1h[:, c].bitcast(F32), ALU.subtract).then_inc(x1_lo, 1)

            def done():
                piece_at(NB - 1, 3, cut_piece)
                add_condition(NB - 1)
                choose(NB - 1)
                weigh(NB - 1)
                places(NB - 1, 1)
                store_places(NB - 1, 1)
                dve.wait_ge(places_all, NB)

            blocks(dve, body, done)
            ffn_dve(dve, S, 0, {1: lambda: tables(dve), 3: lambda: rows_in_ys(dve), 5: lambda: gate_weights(dve)})

            def cut_x(n):
                dve.wait_ge(xg_hi, n)
                tt(xgl[:].rearrange("p k n -> p (k n)"), TX[:],
                   xgh[:].rearrange("p k n -> p (k n)").bitcast(F32), ALU.subtract).then_inc(xg_lo, 1)

            def cut_h(n):
                dve.wait_ge(ht_hi, n)
                tt(hTl[:].rearrange("p k n -> p (k n)"), TH[:],
                   hTh[:].rearrange("p k n -> p (k n)").bitcast(F32), ALU.subtract).then_inc(ht_lo, 1)

            dve.wait_ge(tab_in, 16)
            cut_x(1)
            cut_x(2)
            cut_h(1)
            pairs = value(dve, PAIRS, 0, PAIRS_MAX, 1)

            def rpair(j):
                for s in range(2):
                    t = j * 2 + s
                    cut_x(t + 3)
                    dve.wait_ge(y_ps, t + 2)
                    if not first(j):
                        dve.wait_ge(y_out[s], j * 16)
                    nc.vector.tensor_copy(yo[:, s], YP[:]).then_inc(y_sb, 1)
                    cut_h(t + 2)
            tiles(dve, pairs, rpair)

            def prepare(b, m):
                nc.vector.tensor_copy(gate_fix[:], gate_all[:, ds(b * (TT * TOPK), TT * TOPK)]).then_inc(gate_f, 1)
                dve.wait_ge(gate_f, m + 1)
                dve.wait_ge(xres_in, m * 16 + 16)

            def add_shared(t, of, n, done_):
                if isinstance(of, int) and of == 0:
                    dve.wait_ge(S.sum_ps, t + 1)
                else:
                    dve.wait_ge(F.sum_ps, of * TT - TT + (t + 1))
                if n is not None:
                    dve.wait_ge(acc, n)
                nc.vector.scalar_tensor_tensor(out=xres[:, t], in0=M[t][:], scalar=1.0 / 3, in1=xres[:, t],
                                               op0=ALU.mult, op1=ALU.add).then_inc(done_, 1)

            def add_expert(t, k, n, done_):
                c = t * TOPK + k
                if n is not None:
                    dve.wait_ge(acc, n)
                nc.vector.scalar_tensor_tensor(
                    out=xres[:, t], in0=yb[:, c], scalar=gate_fix[:, c:c + 1], in1=xres[:, t],
                    op0=ALU.mult, op1=ALU.add).then_inc(done_, 1)

            def start_sum(b, m):
                prepare(b, m)
                for t in range(TT):
                    add_shared(t, m, None, acc)

            def end_sum(m):
                dve.wait_ge(y_in, m * (16 * TT * TOPK) + 16 * TT * TOPK)
                for k in range(TOPK):
                    for t in range(TT):
                        add_expert(t, k, m * (2 * TT) + (k * TT + t + 1), acc if k == 0 else comb)

            def last_sum(b, m):
                prepare(b, m)
                dve.wait_ge(y_in, (m + 1) * (16 * TT * TOPK))
                for k in range(TOPK):
                    for t in range(TT):
                        add_expert(t, k, m * (2 * TT) + t + 1 if k > 0 else None, acc)

            def cut_block(b):
                for c in range(KC):
                    dve.wait_ge(xf_hi, b * KC + c + 1)
                    if first(b) and c in (1, 2):
                        dve.wait_ge(y_out[c - 1], pairs * 16)
                    tt(x1l[:, c], x1raw[:, c * T:(c + 1) * T], x1h[:, c].bitcast(F32),
                       ALU.subtract).then_inc(xf_lo, 1)

            cut_block(0)
            start_sum(NB - 1, 0)
            with dve.Fori(0, NB - 2) as b:
                ffn_dve(dve, F, b, {2: lambda: end_sum(b)})
                cut_block(b + 1)
                start_sum(b, b + 1)
            ffn_dve(dve, F, NB - 2, {2: lambda: end_sum(NB - 2), HC - 2: lambda: last_sum(NB - 2, NB - 1)})
            for t in range(TT):
                add_shared(t, NB - 1, (NB - 1) * (2 * TT) + (TT + t + 1), comb)

        @block.tensor
        def _(pe):
            mm = nc.tensor.matmul

            def mm3(o, ah, al, bh, bl, start, stop):
                mm(o, ah, bh, start=start, stop=False)
                mm(o, ah, bl, start=False, stop=False)
                return mm(o, al, bh, start=False, stop=stop)

            def turn8(dst, src, k):
                return nc.tensor.transpose(dst[:, k * 8:(k + 1) * 8], src[:, k * P:(k + 1) * P], ident[0:8, 0:8])

            pe.wait_ge(consts, 3)
            pe.wait_ge(small_in, 16 * 7)
            for k in range(KC):
                last_mm = turn8(K[0], craw, k)
            last_mm.then_inc(p0, 1)
            pe.wait_ge(d0, D_AE)
            for k in range(KC):
                last_mm = turn8(K[1], ae, k)
            last_mm.then_inc(p0, 1)
            pe.wait_ge(d0, D_AET)
            for k in range(KC):
                last_mm = mm(L[0:8, :], actT[:, 1, k], w1c[:, k], start=(k == 0), stop=(k == KC - 1))
            last_mm.then_inc(p0, 1)
            pe.wait_ge(a0, 2)
            for k in range(KC):
                last_mm = turn8(K[0], hc_, k)
            last_mm.then_inc(p0, 1)
            for k in range(KC):
                last_mm = mm(Rb[0:8, 0:E], actT[:, 0, k], rwr[:, KC + k], start=(k == 0), stop=(k == KC - 1))
            last_mm.then_inc(p0, 1)
            pe.wait_ge(d0, D_TBS)
            mm(Rb[:, 64:64 + NB * E], ones[0:8, :], tbs[:].rearrange("p b e -> p (b e)"),
               start=True, stop=True).then_inc(p0, 1)
            for n in range(NCH):
                pe.wait_ge(w2c_in[n % RING], 32 * (n // RING + 1))
                if n >= 2:
                    pe.wait_ge(xw_sb, n - 1)
                for k in range(KC):
                    for q in range(QUADS):
                        last_mm = mm(M[n % 2][32 * q:32 * q + 8, 0:P], actT[:, 2, k], w2c[:, n % RING, k, q * P:(q + 1) * P],
                                     start=(k == 0), stop=(k == KC - 1), tile_position=(0, 32 * q))
                last_mm.then_inc(xw_ps, 1)

            def xtr(b, c):
                pe.wait_ge(x_in[c], b * 16 + 16)
                if c == 0 and not first(b):
                    if isinstance(b, int) and b == 1:
                        pe.wait_ge(xt_lo, 3)
                    else:
                        pe.wait_ge(tok_sb, b * TT - 4)
                elif c == 1 and not first(b):
                    pe.wait_ge(xt_lo, b * KC)
                elif c >= 2 and first(b):
                    pe.wait_ge(xt_lo, c - 1)
                elif c == 2:
                    pe.wait_ge(tok_sb, b * TT - 3)
                elif c == 3:
                    pe.wait_ge(tok_sb, b * TT - 1)
                for t in range(TT):
                    last_mm = nc.tensor.transpose(K[c % 2][:, t * P:(t + 1) * P], xtok[:, t, c * P:(c + 1) * P], ident[:])
                last_mm.then_inc(xt_ps, 1)

            def lay(b, c):
                pe.wait_ge(stk_lo, b * 2 + 2)
                if c > 0 or not first(b):
                    pe.wait_ge(lay_f, b * KC + c)
                mm(L[:], stk[:, 0, c * P:(c + 1) * P], stk[:, 1], start=True, stop=True).then_inc(lay_ps, 1)

            def main(b, c):
                pe.wait_ge(xt_lo, b * KC + c + 1)
                pe.wait_ge(lay_lo, b * KC + c + 1)
                for o in range(KC):
                    if c == 0 and not first(b):
                        pe.wait_ge(x1_f, b * KC + (o - 3))
                    cols = slice(o * P, (o + 1) * P)
                    last_mm = mm3(M[o][:], layh[:, c, cols], layl[:, c, cols], xTh[:, c], xTl[:, c], c == 0, c == KC - 1)
                    if c == KC - 1:
                        last_mm.then_inc(main_ps, 1)

            def tok(b, t):
                pe.wait_ge(x1_f, b * KC + KC)
                if t == 0:
                    pe.wait_ge(*((tok_sb, b * TT) if last(b) else (xt_lo, b * KC + 5)))
                elif t == 1:
                    pe.wait_ge(xt_lo, b * KC + (4 if last(b) else 6))
                elif t == 2:
                    pe.wait_ge(tok_sb, b * TT + 2)
                else:
                    pe.wait_ge(*((tok_sb, b * TT + 1) if last(b) else (xt_lo, b * KC + 7)))
                for o in range(KC):
                    last_mm = nc.tensor.transpose(K[TOK_BANK[t]][:, o * P:(o + 1) * P], x1T[:, o, t * P:(t + 1) * P], ident[:])
                last_mm.then_inc(tok_ps, 1)

            def router(b):
                pe.wait_ge(x1_lo, b * KC + KC)
                if not first(b):
                    pe.wait_ge(pos_rdy, b)
                for k in range(KC):
                    mm(Rb[0:2 * E, :], rwhl[:, k], x1h[:, k], start=(k == 0), stop=False)
                    last_mm = mm(Rb[0:2 * E, :], rwhl[:, k], x1l[:, k], start=False, stop=(k == KC - 1))
                last_mm.then_inc(zt_ps, 1)

            def turn(b):
                pe.wait_ge(zt_sb, b + 1)
                for t in range(TT):
                    last_mm = mm(Rb[:, t * E:(t + 1) * E], zT[:, t * P:(t + 1) * P], sum16[:], start=True, stop=True)
                last_mm.then_inc(z_ps, 1)

            def rank(b):
                pe.wait_ge(masks, b * 2 + 1)
                out = Rb[:, RANKS].rearrange("p (t e) -> p t e", e=E)
                mm(out, upper[:], mk[:], start=True, stop=False)
                for t in range(TT):
                    last_mm = mm(out[:, t + 1:], ones[:], mk[:, t:t + 1].broadcast_to([P, TT - t, E]),
                                 start=False, stop=(t == TT - 1))
                last_mm.then_inc(rank_ps, 1)

            for c in range(2):
                xtr(0, c)
                lay(0, c)

            def body(b, slot):
                main(b, 0)
                xtr(b, 2)
                lay(b, 2)
                if not first(b):
                    tok(b - 1, 2)
                main(b, 1)
                if not first(b):
                    tok(b - 1, 3)
                xtr(b, 3)
                lay(b, 3)
                if not first(b):
                    router(b - 1)
                if not last(b):
                    xtr(b + 1, 0)
                if not first(b):
                    turn(b - 1)
                main(b, 2)
                if not last(b):
                    lay(b + 1, 0)
                main(b, 3)
                if not last(b):
                    xtr(b + 1, 1)
                tok(b, 0)
                if not last(b):
                    lay(b + 1, 1)
                tok(b, 1)
                if not first(b):
                    rank(b - 1)

            def done():
                tok(NB - 1, 2)
                tok(NB - 1, 3)
                router(NB - 1)
                turn(NB - 1)

            blocks(pe, body, done)

            def ffn(S, b, banks, x_ready, between, sum_free, near_end=lambda: None):
                def sums(h):
                    pe.wait_ge(S.g_lo, b * HC + h + 1)
                    for t in range(TT):
                        if h == 0:
                            sum_free(t)
                        rows = slice(t * P, (t + 1) * P)
                        s_ = h % 2
                        last_mm = mm3(M[t][:], gTh[:, s_, rows], gTl[:, s_, rows], w2h[:, h], w2l[:, h], h == 0, h == HC - 1)
                        if h == HC - 1:
                            last_mm.then_inc(S.sum_ps, 1)
                    if h < HC - 1:
                        last_mm.then_inc(S.o_ps, 1)

                for h in range(HC):
                    n = b * HC + h
                    if h >= 2 or banks is None:
                        pe.wait_ge(S.silu, n - 1)
                        pe.wait_ge(S.g_f, n - 1)
                    cols = slice(h * P, (h + 1) * P)
                    for i, (bank, s_) in enumerate(((U[h % 2], S.u_ps), (V[h % 2], S.v_ps))):
                        if h < 2 and banks is not None:
                            banks(h, i)
                        for k in range(KC):
                            if h == 0 and i == 0:
                                x_ready(k)
                            last_mm = mm3(bank[:], w13h[:, i, k, cols], w13l[:, i, k, cols], x1h[:, k], x1l[:, k],
                                          k == 0, k == KC - 1)
                        last_mm.then_inc(s_, 1)
                    if h == 0:
                        between()
                    else:
                        sums(h - 1)
                near_end()
                sums(HC - 1)

            pe.wait_ge(wsl, PIECES)
            def banks_s(h, i):
                pe.wait_ge(tok_sb, NB * TT)
                pe.wait_ge(lay_f, NB * KC)
                if V[h] is Rb and i == 1:
                    pe.wait_ge(pos_rdy, NB)
            def tx(t, slot):
                pe.wait_ge(xr_in[slot], ((t - slot) >> 1) * 16 + 16)
                pe.wait_ge(xg_lo, t)
                for k in range(KC):
                    last_mm = nc.tensor.transpose(TX[:, k * P:(k + 1) * P], xr[:, slot, k * P:(k + 1) * P], ident[:])
                last_mm.then_inc(xg_ps, 1)

            def first_tile():
                pe.wait_ge(tab_in, 16)
                pe.wait_ge(S.silu, HC)
                pe.wait_ge(S.g_f, HC)
                tx(0, 0)

            def between_s():
                rank(NB - 1)
                pe.wait_ge(rank_ps, NB)
                pe.sem_inc(y_ps, 1)
            ffn(S, 0, banks_s, lambda k: pe.wait_ge(x1_lo, NB * KC), between_s,
                lambda t: pe.wait_ge(x1_hi, NB * KC), first_tile)

            def expert(t, m, o, ah, al, ready, free, done_):
                off = value(pe, WOFF, t, WSL)
                need = value(pe, WCNT, t, 2 * E, 1)
                pe.wait_ge(we_lo, need + m)
                ready()
                free()
                for k in range(KC):
                    last_mm = mm3(o, ah[:, k], al[:, k], weh[:, m, ds(off + k * HE, HE)], wel[:, m, ds(off + k * HE, HE)],
                                  k == 0, k == KC - 1)
                last_mm.then_inc(done_, 1)

            def mm1(t):
                expert(t, 0, HP[:], xgh, xgl, lambda: pe.wait_ge(xg_lo, t + 1), lambda: pe.wait_ge(h_g, t), h_ps)

            def mm2(t):
                expert(t, 1, YP[:], hTh, hTl, lambda: pe.wait_ge(ht_lo, t + 1), lambda: pe.wait_ge(y_sb, t), y_ps)

            def th(t):
                pe.wait_ge(h_g, t + 1)
                pe.wait_ge(ht_lo, t)
                for k in range(KC):
                    last_mm = nc.tensor.transpose(TH[:, k * P:(k + 1) * P], hg[:, k * P:(k + 1) * P], ident[:])
                last_mm.then_inc(ht_ps, 1)

            mm1(0)
            tx(1, 1)
            th(0)
            pairs = value(pe, PAIRS, 0, PAIRS_MAX, 1)

            def rpair(j):
                for s in range(2):
                    t = j * 2 + s
                    mm1(t + 1)
                    tx(t + 2, s)
                    mm2(t)
                    th(t + 1)
            tiles(pe, pairs, rpair)

            pe.wait_ge(xg_lo, pairs * 2 + 2)
            pe.wait_ge(ht_lo, pairs * 2 + 1)
            pe.wait_ge(h_g, pairs * 2 + 1)
            pe.wait_ge(y_sb, pairs * 2)

            def fblock(b):
                ffn(F, b, (lambda h, i: None) if first(b) else None, lambda k: pe.wait_ge(xf_lo, b * KC + k + 1),
                    lambda: None, lambda t: pe.wait_ge(acc, b * (2 * TT) + t + 1))
            fblock(0)
            with pe.Fori(1, NB - 1) as b:
                fblock(b)


_INS = ['x', 'cond_1024', 'L0_cond_base_layer', 'L0_cond_w1', 'L0_cond_b1', 'L0_cond_w2', 'L0_cond_b2', 'L0_cond_ln_g',
        'L0_cond_ln_b', 'L1_cond_router_W', 'L1_cond_router_bias', 'L1_cond_w1', 'L1_cond_w3', 'L1_cond_w2',
        'L1_cond_W1e', 'L1_cond_W2e']
_OUTS = [((8, 512, 512), 'float32')]


def kernel(**inputs):
    import numpy as _np
    import concourse.bacc as _bacc
    from concourse import mybir as _mybir
    from concourse.bass_utils import run_bass_kernel_spmd as _run

    nc = _bacc.Bacc("TRN2", target_bir_lowering=False, num_devices=1)
    arrays, args = {}, []
    for name in _INS:
        a = _np.ascontiguousarray(inputs[name])
        arrays[f"in_{name}_dram"] = a
        args.append(nc.dram_tensor(f"in_{name}_dram", a.shape, _mybir.dt.from_np(a.dtype), kind="ExternalInput").ap())
    for i, (shape, dtype) in enumerate(_OUTS):
        dt = _mybir.dt.from_np(_np.dtype(dtype))
        args.append(nc.dram_tensor(f"out_{i}_dram", shape, dt, kind="ExternalOutput").ap())
    build(nc, *args)
    r = _run(nc, [arrays], core_ids=[0])
    got = tuple(r.results[0][f"out_{i}_dram"] for i in range(len(_OUTS)))
    return got[0]
```
